# Optimizing a Trainium2 kernel written in Bass

```python
import numpy as np
import jax
import jax.numpy as jnp

def _softmax(x, axis=-1):
    return jax.nn.softmax(x, axis=axis)

def _gelu(x):
    return jax.nn.gelu(x, approximate=True)

def _silu(x):
    return jax.nn.silu(x)

def _sigmoid(x):
    return jax.nn.sigmoid(x)

def _layernorm(x, axis=-1, eps=1e-05):
    m = jnp.mean(x, axis=axis, keepdims=True)
    v = jnp.var(x, axis=axis, keepdims=True)
    return (x - m) / jnp.sqrt(v + eps)

def _scatter_add(tgt, idx, src, axis=0):
    return tgt.at[idx].add(src)

def _segment_sum(src, seg, n):
    return jax.ops.segment_sum(src, seg, n)
kernel_name = 'mk_flamingo_gated_d1_seqx_r4_cf25af'

def setup_inputs(seed: int=0):
    np.random.seed(seed)
    _w = jnp.asarray

    def _rec_inputs():
        import jax
        import jax.numpy as jnp
        _rk = jax.random.key(seed)
        x = -0.0002928 + 1 * jax.random.normal(jax.random.fold_in(_rk, 1), (16, 512, 256), jnp.float32)
        _lenS = 512 - jax.random.randint(jax.random.fold_in(_rk, 7), (16,), 0, max(1, 512 // 4) + 1, jnp.int32)
        _lenS2 = 1601 - jax.random.randint(jax.random.fold_in(_rk, 8), (16,), 0, max(1, 1601 // 4) + 1, jnp.int32)
        _ctx_512P = jax.random.normal(jax.random.fold_in(_rk, 11), (16, 16, 128), jnp.float32)
        _ctx_512c = jax.random.dirichlet(jax.random.fold_in(_rk, 511), 0.3 * jnp.ones((16,), jnp.float32), (16, 1601))
        _ctx_512t = jnp.einsum('bsk,bkd->bsd', _ctx_512c, _ctx_512P)
        _ctx_512t = _ctx_512t * jax.lax.rsqrt(jnp.mean(jnp.square(_ctx_512t)) + 1e-12) * 0.953939
        ctx_512 = 0.00222621 + 0.99962 * (_ctx_512t + 0.3 * jax.random.normal(jax.random.fold_in(_rk, 611), (16, 1601, 128), jnp.float32))
        _g = jax.random.normal(jax.random.fold_in(_rk, 9001), (2, 1), jnp.float32)
        _g = jnp.sign(_g) * jnp.maximum(jnp.abs(_g), 1.0) + (_g == 0) * 1.0
        g_xattn = _g[0]
        g_ffn = _g[1]
        return (x, ctx_512, g_xattn, g_ffn)
    x, ctx_512, g_xattn, g_ffn = _rec_inputs()

    def _L0_xattn_setup():
        import jax, jax.numpy as jnp
        import numpy as np
        B, T, TC, C, CC, H = (2, 512, 128, 256, 128, 16)
        D = C // H

        def _heads(t):
            b, l, _ = t.shape
            return t.reshape(b, l, H, D).transpose(0, 2, 1, 3)
        key = jax.random.key(seed)
        ks = jax.random.split(key, 18)
        w = lambda k, i, o: jax.random.normal(k, (i, o), jnp.float32) / np.sqrt(i).astype(np.float32)
        return {'x': jax.random.normal(ks[0], (B, T, C), jnp.float32), 'cross_input': jax.random.normal(ks[1], (B, TC, CC), jnp.float32), 'Wk': w(ks[2], C, C), 'bk': jnp.zeros((C,), jnp.float32), 'Wq': w(ks[3], C, C), 'bq': jnp.zeros((C,), jnp.float32), 'Wv': w(ks[4], C, C), 'bv': jnp.zeros((C,), jnp.float32), 'Wck': w(ks[5], CC, C), 'bck': jnp.zeros((C,), jnp.float32), 'Wcq': w(ks[6], C, C), 'bcq': jnp.zeros((C,), jnp.float32), 'Wcv': w(ks[7], CC, C), 'bcv': jnp.zeros((C,), jnp.float32), 'Wp': w(ks[8], C, C), 'bp': jnp.zeros((C,), jnp.float32)}
    _L0_xattn_all = _L0_xattn_setup()
    _L0_xattn_in = {k: v for k, v in _L0_xattn_all.items() if k in ('Wk', 'bk', 'Wq', 'bq', 'Wv', 'bv', 'Wck', 'bck', 'Wcq', 'bcq', 'Wcv', 'bcv', 'Wp', 'bp')}
    del _L0_xattn_all

    def _L0_ffn_setup():
        import jax, jax.numpy as jnp
        import numpy as np
        TOP_K = 4
        CAP_FACTOR = 4

        def swiglu(x, w1, w2, w3):
            return jax.nn.silu(x @ w1) * (x @ w3) @ w2
        key = jax.random.key(seed)
        ks = jax.random.split(key, 8)
        B, S, D, H, E = (2, 512, 256, 128, 32)
        Hs = 2 * H
        sd = lambda *sh: 1.0 / np.sqrt(sh[-2])
        x = jax.random.normal(ks[0], (B, S, D), dtype=jnp.float32)
        Wg = jax.random.normal(ks[1], (D, E), dtype=jnp.float32) * (1.0 / np.sqrt(D))
        W1 = jax.random.normal(ks[2], (E, D, H), dtype=jnp.float32) * (1.0 / np.sqrt(D))
        W3 = jax.random.normal(ks[3], (E, D, H), dtype=jnp.float32) * (1.0 / np.sqrt(D))
        W2 = jax.random.normal(ks[4], (E, H, D), dtype=jnp.float32) * (1.0 / np.sqrt(H))
        Ws1 = jax.random.normal(ks[5], (D, Hs), dtype=jnp.float32) * (1.0 / np.sqrt(D))
        Ws3 = jax.random.normal(ks[6], (D, Hs), dtype=jnp.float32) * (1.0 / np.sqrt(D))
        Ws2 = jax.random.normal(ks[7], (Hs, D), dtype=jnp.float32) * (1.0 / np.sqrt(Hs))
        return {'x': x, 'Wg': Wg, 'W1': W1, 'W2': W2, 'W3': W3, 'Ws1': Ws1, 'Ws2': Ws2, 'Ws3': Ws3}
    _L0_ffn_all = _L0_ffn_setup()
    _L0_ffn_in = {k: v for k, v in _L0_ffn_all.items() if k in ('Wg', 'W1', 'W2', 'W3', 'Ws1', 'Ws2', 'Ws3')}
    del _L0_ffn_all
    return {'x': x, 'ctx_512': ctx_512, 'g_xattn': g_xattn, 'g_ffn': g_ffn, 'L0_xattn_Wk': _L0_xattn_in['Wk'], 'L0_xattn_bk': _L0_xattn_in['bk'], 'L0_xattn_Wq': _L0_xattn_in['Wq'], 'L0_xattn_bq': _L0_xattn_in['bq'], 'L0_xattn_Wv': _L0_xattn_in['Wv'], 'L0_xattn_bv': _L0_xattn_in['bv'], 'L0_xattn_Wck': _L0_xattn_in['Wck'], 'L0_xattn_bck': _L0_xattn_in['bck'], 'L0_xattn_Wcq': _L0_xattn_in['Wcq'], 'L0_xattn_bcq': _L0_xattn_in['bcq'], 'L0_xattn_Wcv': _L0_xattn_in['Wcv'], 'L0_xattn_bcv': _L0_xattn_in['bcv'], 'L0_xattn_Wp': _L0_xattn_in['Wp'], 'L0_xattn_bp': _L0_xattn_in['bp'], 'L0_ffn_Wg': _L0_ffn_in['Wg'], 'L0_ffn_W1': _L0_ffn_in['W1'], 'L0_ffn_W2': _L0_ffn_in['W2'], 'L0_ffn_W3': _L0_ffn_in['W3'], 'L0_ffn_Ws1': _L0_ffn_in['Ws1'], 'L0_ffn_Ws2': _L0_ffn_in['Ws2'], 'L0_ffn_Ws3': _L0_ffn_in['Ws3']}

def reference(x, ctx_512, g_xattn, g_ffn, L0_xattn_Wk, L0_xattn_bk, L0_xattn_Wq, L0_xattn_bq, L0_xattn_Wv, L0_xattn_bv, L0_xattn_Wck, L0_xattn_bck, L0_xattn_Wcq, L0_xattn_bcq, L0_xattn_Wcv, L0_xattn_bcv, L0_xattn_Wp, L0_xattn_bp, L0_ffn_Wg, L0_ffn_W1, L0_ffn_W2, L0_ffn_W3, L0_ffn_Ws1, L0_ffn_Ws2, L0_ffn_Ws3):
    import jax
    import jax.numpy as jnp

    def _L0_xattn_ref(x, cross_input, Wk, bk, Wq, bq, Wv, bv, Wck, bck, Wcq, bcq, Wcv, bcv, Wp, bp):
        import jax, jax.numpy as jnp
        import numpy as np
        B, T, TC, C, CC, H = (2, 512, 128, 256, 128, 16)
        D = C // H

        def _heads(t):
            b, l, _ = t.shape
            return t.reshape(b, l, H, D).transpose(0, 2, 1, 3)
        scale = np.float32(1.0 / np.sqrt(D))
        q = _heads(x @ Wq + bq)
        k = _heads(x @ Wk + bk)
        v = _heads(x @ Wv + bv)
        att = jnp.einsum('bhqd,bhkd->bhqk', q, k) * scale
        causal = jnp.tril(jnp.ones((T, T), bool))
        att = jnp.where(causal[None, None], att, -jnp.inf)
        y = jnp.einsum('bhqk,bhkd->bhqd', jax.nn.softmax(att, axis=-1), v)
        qc = _heads(x @ Wcq + bcq)
        kc = _heads(cross_input @ Wck + bck)
        vc = _heads(cross_input @ Wcv + bcv)
        attc = jnp.einsum('bhqd,bhkd->bhqk', qc, kc) * scale
        y = y + jnp.einsum('bhqk,bhkd->bhqd', jax.nn.softmax(attc, axis=-1), vc)
        y = y.transpose(0, 2, 1, 3).reshape(x.shape[0], T, C)
        return y @ Wp + bp

    def _L0_ffn_ref(x, Wg, W1, W2, W3, Ws1, Ws2, Ws3):
        import jax, jax.numpy as jnp
        import numpy as np
        TOP_K = 4
        CAP_FACTOR = 4

        def swiglu(x, w1, w2, w3):
            return jax.nn.silu(x @ w1) * (x @ w3) @ w2
        B, S, D = x.shape
        E = Wg.shape[1]
        T = B * S
        xf = x.reshape(T, D)
        scores = jax.nn.softmax(xf @ Wg, axis=-1)
        weights, indices = jax.lax.top_k(scores, TOP_K)
        P = T * TOP_K
        pair_expert = indices.reshape(-1)
        pair_token = jnp.repeat(jnp.arange(T), TOP_K)
        pair_weight = weights.reshape(-1).astype(xf.dtype)
        C = CAP_FACTOR * P // E
        y = jnp.zeros_like(xf)
        for e in range(E):
            pos = jnp.nonzero(pair_expert == e, size=C, fill_value=P)[0]
            valid = pos < P
            safe = jnp.minimum(pos, P - 1)
            tok = jnp.where(valid, pair_token[safe], 0)
            w = jnp.where(valid, pair_weight[safe], 0.0)
            xg = xf[tok]
            out = swiglu(xg, W1[e], W2[e], W3[e]) * w[:, None]
            y = y.at[tok].add(out)
        z = swiglu(xf, Ws1, Ws2, Ws3)
        return (y + z).reshape(B, S, D)
    x = x + jnp.tanh(g_xattn[0]) * _L0_xattn_ref(_layernorm(x, axis=-1), ctx_512, L0_xattn_Wk, L0_xattn_bk, L0_xattn_Wq, L0_xattn_bq, L0_xattn_Wv, L0_xattn_bv, L0_xattn_Wck, L0_xattn_bck, L0_xattn_Wcq, L0_xattn_bcq, L0_xattn_Wcv, L0_xattn_bcv, L0_xattn_Wp, L0_xattn_bp)
    x = x + jnp.tanh(g_ffn[0]) * _L0_ffn_ref(_layernorm(x, axis=-1), L0_ffn_Wg, L0_ffn_W1, L0_ffn_W2, L0_ffn_W3, L0_ffn_Ws1, L0_ffn_Ws2, L0_ffn_Ws3)
    return x

_drawn_inputs = setup_inputs


def setup_inputs(seed=0):
    import zlib

    import numpy as np

    out = dict(_drawn_inputs(seed))
    spreads = {'L0_xattn_bk': (0.0, 0.8),
     'L0_xattn_bq': (0.0, 0.591),
     'L0_xattn_bv': (0.0, 0.1),
     'L0_xattn_bck': (0.0, 0.8),
     'L0_xattn_bcq': (0.0, 0.396),
     'L0_xattn_bcv': (0.0, 0.1),
     'L0_xattn_bp': (0.0, 0.1)}
    factors = {}
    for name, (base, spread) in spreads.items():
        noise = np.random.default_rng([zlib.crc32(name.encode()), seed]).standard_normal(out[name].shape)
        drawn = base * np.exp(spread * noise) if base else spread * noise
        out[name] = jnp.asarray(drawn.astype(out[name].dtype))
    for name, factor in factors.items():
        out[name] = (out[name] * factor).astype(out[name].dtype)
    return out
```

```python
from contextlib import ExitStack

import numpy as np

import concourse.bass as bass
from concourse import mybir

F32 = mybir.dt.float32
F32R = mybir.dt.float32r
BF16 = mybir.dt.bfloat16
I32 = mybir.dt.int32
U32 = mybir.dt.uint32
ALU = mybir.AluOpType
ACT = mybir.ActivationFunctionType
AX = mybir.AxisListType

ENGINES = ("pe", "act", "dve", "pool", "sp")


class Phase:

    def __init__(self, before=None):
        self.steps = {e: [] for e in ENGINES}
        self.count = {}
        self.waited = {}
        self.named = {}
        if before is not None:
            self.named = {k: (s, v - before.count.get(s, 0)) for k, (s, v) in before.named.items()}

    def do(self, engine, fn, name=None, sem=None, by=1, alone=False):
        sem = sem or engine
        if name is not None:
            self.count[sem] = self.count.get(sem, 0) + by
            self.named[name] = (sem, self.count[sem])
        self.steps[engine].append(("do", fn, sem if name is not None else None, by, alone or engine in ("pool", "sp")))

    def wait(self, engine, *names):
        for name in names:
            if name not in self.named:
                continue
            sem, value = self.named[name]
            if self.waited.get((engine, sem), -10**9) >= value:
                continue
            self.waited[(engine, sem)] = value
            self.steps[engine].append(("wait", sem, value))

    def run(self, engine, eng, sems, base, batch):
        pending = False
        for step in self.steps[engine]:
            if step[0] == "wait":
                value = base.get(step[1], 0) + step[2]
                if isinstance(value, int) and value <= 0:
                    continue
                eng.wait_ge(sems[step[1]], value)
                pending = not isinstance(value, int)
                if pending and engine == "sp":
                    eng.sem_inc(sems["spare_sp"], 1)
                    pending = False
            else:
                if pending and step[4]:
                    eng.sem_inc(sems["spare_" + engine], 1)
                pending = False
                ins = step[1](eng, batch)
                if step[2] is not None:
                    ins.then_inc(sems[step[2]], step[3])


def total(*phases):
    out = {}
    for ph in phases:
        for s, n in ph.count.items():
            out[s] = out.get(s, 0) + n
    return out


def build_attention(nc, B, x, ctx_t, w, scr):
    T, C, TC, CC, H, D = 512, 256, 1601, 128, 16, 16
    E = w["Wg"].shape[1]
    NQ = T // 128
    KC = C // 128
    NCT = (TC + 127) // 128
    REST = TC - 128 * (NCT - 1)
    VE = D + 1
    VW = 8 * VE + 16
    QP, KP = (0, 0, 1, 1, 0, 2), (0, 1, 0, 1, 2, 0)
    KR = D * len(QP)
    SCALE = 1.0 / float(np.sqrt(D))
    EPS = 1e-5

    with ExitStack() as ctx:
        def sb(name, shape, dt=F32):
            return ctx.enter_context(nc.sbuf_tensor(name, shape, dt))

        wq = sb("wq", [128, KC, C])
        wk = sb("wk", [128, KC, C])
        wv = sb("wv", [128, KC, C])
        wcq = sb("wcq", [128, KC, C])
        wck = sb("wck", [128, C])
        wcv = sb("wcv", [128, C])
        wp = sb("wp", [128, 4, C])
        wg = sb("wg", [128, KC, E])
        ws1 = sb("ws1", [128, KC, C])
        ws3 = sb("ws3", [128, KC, C])
        ws2 = sb("ws2", [128, KC, C])
        bcol = sb("bcol", [128, 4, 2])
        bvb = sb("bvb", [128, C])
        bcvb = sb("bcvb", [128, C])
        bpt = sb("bpt", [128, C])
        gates = sb("gates", [128, 2])
        ident = sb("ident", [128, 128])
        identb = sb("identb", [128, 128], BF16)
        maskb = sb("maskb", [128, 128], BF16)
        qst = [sb(f"qst{c}", [128, 8, 2 * T], BF16) for c in range(2)]
        kst = [sb(f"kst{c}", [128, 8, T + TC + 1], BF16) for c in range(2)]
        vt = [sb(f"vt{c}", [128, NCT + NQ, VW]) for c in range(2)]
        SW = T + TC - 2 * 512 + 1
        split = [sb(f"split{i}", [128, 3 * SW], BF16) for i in range(2)]
        rest = sb("rest", [128, 2, 512])
        prob = sb("prob", [128, 2, 4, 512])
        xa = sb("xa", [128, NQ, C])
        xt = sb("xt", [128, KC, T])
        ct = sb("ct", [128, TC])
        yg = sb("yg", [128, 4, T])
        oc = sb("oc", [128, 2, T])
        dsum = sb("dsum", [128, 32])
        den = sb("den", [128, 2, T])
        stat = sb("stat", [128, NQ, 6])
        mv = sb("mv", [128, NQ, 2])
        rstd = sb("rstd", [128, NQ])
        var = sb("var", [128, NQ])
        newt = sb("newt", [128, NQ])
        lgt = sb("lgt", [128, NQ, E])
        pmx = sb("pmx", [128, 8, NQ, 4])
        mc = sb("mc", [128, 64])
        mr = sb("mr", [64, 2, 128], BF16)
        ps = ctx.enter_context(nc.psum_tensor("scores", [128, 4, 512], F32))
        pm = ctx.enter_context(nc.psum_tensor("ring", [128, 3, 512], F32))
        po = ctx.enter_context(nc.psum_tensor("outs", [128, 512], F32))
        xr = ct[:, 0:NQ * C].rearrange("p (q c) -> p q c", c=C)
        act_t, sig_t = (s[:, 0:4 * T].bitcast(F32).rearrange("p (m n) -> p m n", m=2) for s in split)

        names = list(ENGINES) + ["w", "wz", "x", "xr", "ctx", "st_q", "st_ck0", "st_ck3", "wr0", "wr1", "mrow0", "mrow1",
                                 "dn1", "dc", "dn2", "den", "xn_out", "lg_out", "x1_out"]
        names += [f"spare_{e}" for e in ENGINES]
        sems = {n: ctx.enter_context(nc.semaphore(f"s_{n}")) for n in names}

        class Ring:
            n = 0

        ring = Ring()

        def bank(ph, free):
            k = ring.n % 3
            ring.n += 1
            ph.wait("pe", f"ring{k}")
            ph.ring = k
            return k

        def freed(ph, k, name):
            ph.named[f"ring{k}"] = ph.named[name]

        def load_weights(ph):
            def ld(dst, src, **kw):
                ph.do("sp", lambda e, b: e.dma_start(dst, src, **kw), "w", sem="w", by=16)
            for dst, src in ((wq, w["Wq"]), (wk, w["Wk"]), (wv, w["Wv"]), (wcq, w["Wcq"]),
                             (ws1, w["Ws1"]), (ws3, w["Ws3"]), (ws2, w["Ws2"]), (wg, w["Wg"])):
                ld(dst[:, :, :], src.rearrange("(k p) n -> p k n", p=128))
            ld(wck[:, :], w["Wck"])
            ld(wcv[:, :], w["Wcv"])
            for i, n in enumerate(("bq", "bk", "bcq", "bck")):
                ld(bcol[:, i, :], w[n].rearrange("(c p) -> p c", p=128), allow_slow_non_contiguous=True)
            ld(bvb[:, :], w["bv"].partition_broadcast(128))
            ld(bcvb[:, :], w["bcv"].partition_broadcast(128))
            ld(bpt[:, :], w["bp"].partition_broadcast(128))
            ld(gates[:, 0:1], w["g_xattn"].partition_broadcast(128))
            ld(gates[:, 1:2], w["g_ffn"].partition_broadcast(128))
            ph.do("pool", lambda e, b: e.memset(ident[:, :], 0.0), "c0")
            ph.do("pool", lambda e, b: e.memset(maskb[:, :], 0.0), "c1")
            ph.do("pool", lambda e, b: e.memset(wp[:, :, :], 0.0), "c2")
            ph.wait("pool", "c0", "c1")
            ph.do("pool", lambda e, b: e.affine_select(
                out=ident[:, :], in_=ident[:, :], compare_op=ALU.not_equal, fill=1.0, base=0,
                pattern=[[-1, 128]], channel_multiplier=1), "ident")
            ph.do("pool", lambda e, b: e.affine_select(
                out=maskb[:, :], in_=maskb[:, :], compare_op=ALU.is_ge, fill=-1e30, base=0,
                pattern=[[-1, 128]], channel_multiplier=1), "mask")
            ph.wait("pool", "ident")
            ph.do("pool", lambda e, b: e.tensor_copy(identb[:, :], ident[:, :]), "identb")
            ph.wait("pool", "identb")
            for c in range(2):
                ph.do("dve", lambda e, b, c=c: e.memset(vt[c][:, :, :], 1.0), "vt_ones")
                ph.do("pool", lambda e, b, c=c: e.memset(kst[c][96:128, :, :], 1.0), "st_ones")
                ph.wait("pool", "st_ones")
            ph.wait("sp", "c2")
            for ch in range(2):
                for v in range(2):
                    for j in range(4):
                        h = ch * 8 + 4 * (j % 2) + 2 * v + j // 2
                        ph.do("sp", lambda e, b, g=2 * ch + v, j=j, h=h: e.dma_start(
                            wp[32 * j:32 * j + D, g, :], w["Wp"][h * D:(h + 1) * D, :]), "w", sem="w", by=16)
            ph.wait("act", "w")
            ph.do("act", lambda e, b: e.activation(gates[:, :], gates[:, :], ACT.Tanh), "gates")
            ph.wait("dve", "w", "gates")
            ph.do("dve", lambda e, b: e.tensor_scalar(bpt[:, :], bpt[:, :], gates[:, 0:1], None, ALU.mult), "bpt")
            ph.wait("pe", "w", "identb", "mask")

        def load_x(ph, d):
            ph.wait("sp", "xn2_t", "xn_out", "ln1_t")
            ph.do("sp", lambda e, b: e.dma_start(xa[:, :, :], x[b + d].rearrange("(q p) c -> p q c", p=128)),
                  "x", sem="x", by=16)

        def load_ctx(ph, d):
            ph.wait("sp", "ct_read", "x1_out")
            ph.do("sp", lambda e, b: e.dma_start(ct[:, :], ctx_t[b + d][:, 0:TC]), "ctx", sem="ctx", by=16)

        def row_stats(ph, src, got):
            ph.wait("dve", *got)
            for q in range(NQ):
                ph.do("dve", lambda e, b, q=q: e.bn_stats(stat[:, q, :], src[:, q, :]), "ln_a")
            ph.wait("dve", "ln_a")
            for q in range(NQ):
                ph.do("dve", lambda e, b, q=q: e.bn_aggr(mv[:, q, :], stat[:, q, :]), "ln_b", alone=True)
            ph.wait("dve", "ln_b")
            ph.do("dve", lambda e, b: e.tensor_scalar(var[:, :], mv[:, :, 1], EPS, None, ALU.add), "ln_c")
            ph.wait("dve", "ln_c", "rstd")
            ph.do("dve", lambda e, b: e.tensor_scalar(
                rstd[:, :].bitcast(I32), var[:, :].bitcast(I32), -0.5, float(0x5F3759DF), ALU.mult, ALU.add), "guess")
            ph.wait("pool", "guess")
            for _ in range(4):
                ph.do("pool", lambda e, b: e.tensor_tensor(newt[:, :], rstd[:, :], rstd[:, :], ALU.mult), "newt")
                ph.wait("pool", "newt")
                ph.do("pool", lambda e, b: e.tensor_tensor(newt[:, :], newt[:, :], var[:, :], ALU.mult), "newt")
                ph.wait("pool", "newt")
                ph.do("pool", lambda e, b: e.tensor_scalar(newt[:, :], newt[:, :], -0.5, 1.5, ALU.mult, ALU.add), "newt")
                ph.wait("pool", "newt")
                ph.do("pool", lambda e, b: e.tensor_tensor(rstd[:, :], rstd[:, :], newt[:, :], ALU.mult), "rstd")
                ph.wait("pool", "rstd")

        def normalise(ph, src, dst, out):
            ph.wait("dve", "rstd")
            for q in range(NQ):
                ph.do("dve", lambda e, b, q=q: e.tensor_scalar(
                    dst[:, q, :], src[:, q, :], mv[:, q, 0:1], rstd[:, q:q + 1], ALU.subtract, ALU.mult), out)

        def transpose_item(src, ready, readers, done, kc):
            def item(ph):
                k = bank(ph, "act")
                ph.wait("pe", ready)
                for q in range(NQ):
                    ph.do("pe", lambda e, b, q=q: e.transpose(
                        pm[:, k, 128 * q:128 * q + 128], src[:, q, 128 * kc:128 * kc + 128], ident[:, :]),
                        done if q == NQ - 1 else None)
                ph.wait("act", done, *readers)
                ph.do("act", lambda e, b: e.copy(xt[:, kc, :], pm[:, k, :]), "xt")
                freed(ph, k, "xt")
            return item

        pieces = [0]
        parts = [0]

        def split_item(ch, kind):
            i, wt, n0, n, at = {
                "cq": (2, wcq, 0, T, 0), "q": (0, wq, 0, T, T),
                "k": (1, wk, 0, T, 0), "ck0": (3, wck, 0, 512, T),
                "ck1": (3, wck, 512, 512, 0), "ck2": (3, wck, 1024, 512, 512), "ck3": (3, wck, 1536, TC - 1536, 1024)}[kind]
            first = kind in ("cq", "k", "ck1")
            piece = {"q": (qst, 0, 2 * T), "ck0": (kst, 0, 2 * T), "ck3": (kst, 2 * T, T + TC - 2 * T)}.get(kind)

            def item(ph):
                k = bank(ph, "dve")
                if first:
                    pieces[0] += 1
                s = pieces[0] % 2
                cs = slice(128 * ch, 128 * ch + 128)
                if i == 3:
                    ph.wait("pe", "ctx")
                    ph.do("pe", lambda e, b: e.matmul(pm[:, k, 0:n], wck[:, cs], ct[:, n0:n0 + n],
                                                      start=True, stop=True), "ct_read")
                    done = "ct_read"
                else:
                    ph.wait("pe", "xt")
                    for kc in range(KC):
                        ph.do("pe", lambda e, b, kc=kc: e.matmul(pm[:, k, 0:n], wt[:, kc, cs], xt[:, kc, :],
                                                                 start=kc == 0, stop=kc == KC - 1),
                              "xt_read" if kc == KC - 1 else None)
                    done = "xt_read"
                bias = bcol[:, i, ch:ch + 1]
                part = [split[s][:, r * SW + at:r * SW + at + n] for r in range(3)]
                ri = parts[0] % 2
                parts[0] += 1
                ph.wait("act", done, f"wr{s}", "z_read")
                ph.do("act", lambda e, b: e.activation(part[0], pm[:, k, 0:n], ACT.Identity, bias=bias), "part0")
                ph.wait("dve", "part0", done, f"part2_{ri}")
                ph.do("dve", lambda e, b: e.scalar_tensor_tensor(
                    out=rest[:, ri, 0:n], in0=pm[:, k, 0:n], scalar=bias, in1=part[0],
                    op0=ALU.add, op1=ALU.subtract), "rest")
                freed(ph, k, "rest")
                ph.wait("dve", "rest", f"wr{s}", "z_read")
                ph.do("dve", lambda e, b: e.tensor_copy(part[1], rest[:, ri, 0:n]), "part1")
                ph.wait("dve", "part1")
                ph.do("dve", lambda e, b: e.tensor_tensor(part[2], rest[:, ri, 0:n], part[1], ALU.subtract),
                      f"part2_{ri}")
                ph.named["part2"] = ph.named[f"part2_{ri}"]
                if piece is None:
                    return
                dst, c0, cn = piece
                ph.wait("sp", "part2", f"slot{s}")
                ph.do("sp", lambda e, b: e.dma_start(
                    scr["parts"][s][:, :, 0:cn].rearrange("k p c -> p k c"),
                    split[s][:, :].rearrange("p (k c) -> p k c", k=3)[:, :, 0:cn]), f"wr{s}", sem=f"wr{s}", by=16)
                ph.wait("sp", f"wr{s}", f"scores{ch}", f"mx{ch}", "st_ones", f"st_{kind}")
                for r, src in enumerate(KP if dst is kst else QP):
                    ph.do("sp", lambda e, b, r=r, src=src: e.dma_start(
                        dst[ch][D * r:D * r + D, :, c0:c0 + cn],
                        scr["parts"][s][src][:, 0:cn].rearrange("(h d) c -> d h c", d=D)),
                        f"st_{kind}", sem=f"st_{kind}", by=16)
                ph.named[f"slot{s}"] = ph.named[f"st_{kind}"]
                ph.named[f"{kind}_{ch}"] = ph.named[f"st_{kind}"]
            return item

        def value_item(ch, k0, nk):
            def item(ph):
                k = bank(ph, "dve")
                cs = slice(128 * ch, 128 * ch + 128)
                rows = 128
                if k0 >= NCT:
                    ph.wait("pe", "xt")
                    for q in range(NQ):
                        for kc in range(KC):
                            ph.do("pe", lambda e, b, q=q, kc=kc: e.matmul(
                                pm[:, k, 128 * q:128 * q + 128], xt[:, kc, 128 * q:128 * q + 128], wv[:, kc, cs],
                                start=kc == 0, stop=kc == KC - 1), "xt_read" if q == NQ - 1 and kc == KC - 1 else None)
                    done, bb = "xt_read", bvb
                else:
                    ph.wait("pe", "ctx")
                    for i in range(nk):
                        r0 = 128 * (k0 + i)
                        rows = min(128, TC - r0)
                        ph.do("pe", lambda e, b, i=i, r0=r0, rows=rows: e.matmul(
                            pm[0:rows, k, 128 * i:128 * i + 128], ct[:, r0:r0 + rows], wcv[:, cs],
                            start=True, stop=True), "ct_read" if i == nk - 1 else None)
                    done, bb = "ct_read", bcvb
                ph.wait("dve", done, f"values{ch}", "w", "vt_ones")
                for i in range(nk):
                    ph.do("dve", lambda e, b, i=i: e.tensor_tensor(
                        vt[ch][0:rows, k0 + i, 0:8 * VE].rearrange("p (h e) -> p h e", e=VE)[:, :, 0:D],
                        pm[0:rows, k, 128 * i:128 * i + 128].rearrange("p (h d) -> p h d", d=D),
                        bb[0:rows, cs].rearrange("p (h d) -> p h d", d=D), ALU.add), "vt")
                freed(ph, k, "vt")
            return item

        def project_items(ch):
            v = [value_item(ch, 4 * i, min(4, NCT - 4 * i)) for i in range(4)]
            p = {k: split_item(ch, k) for k in ("cq", "q", "k", "ck0", "ck1", "ck2", "ck3")}
            return [p["cq"], p["q"], p["k"], p["ck0"], p["ck1"], p["ck2"], p["ck3"]], v + [value_item(ch, NCT, NQ)]

        def max_items(ch):
            out = []

            def reduce(ph, k, done, dst, src, name="mx_part"):
                ph.wait("dve", done)
                ph.do("dve", lambda e, b: e.tensor_reduce(dst, src, AX.X, ALU.max), name)
                freed(ph, k, name)

            def cross(hl, qt, part):
                def item(ph):
                    k = bank(ph, "dve")
                    ph.wait("pe", f"q_{ch}", f"ck0_{ch}", f"ck3_{ch}")
                    ph.do("pe", lambda e, b: e.matmul(
                        pm[:, k, :], qst[ch][0:KR, hl, 128 * qt:128 * qt + 128],
                        kst[ch][0:KR, hl, T + 512 * part:T + 512 * part + 512], start=True, stop=True), f"mx{ch}")
                    reduce(ph, k, f"mx{ch}", pmx[:, hl, qt, part:part + 1], pm[:, k, :])
                return item

            def cross_rest(hl):
                def item(ph):
                    k = bank(ph, "dve")
                    ph.wait("pe", f"q_{ch}", f"ck0_{ch}", f"ck3_{ch}")
                    for qt in range(NQ):
                        ph.do("pe", lambda e, b, qt=qt: e.matmul(
                            pm[:, k, 66 * qt:66 * qt + 66], qst[ch][0:KR, hl, 128 * qt:128 * qt + 128],
                            kst[ch][0:KR, hl, T + TC - 66:T + TC], start=True, stop=True), f"mx{ch}" if qt == NQ - 1 else None)
                    reduce(ph, k, f"mx{ch}", pmx[:, hl, :, 3], pm[:, k, 0:66 * NQ].rearrange("p (q n) -> p q n", q=NQ))
                return item

            def own(hl, qt):
                def item(ph):
                    k = bank(ph, "dve")
                    n = 128 * (qt + 1)
                    ph.wait("pe", f"q_{ch}", f"ck0_{ch}")
                    ph.do("pe", lambda e, b: e.matmul(
                        pm[:, k, 0:n], qst[ch][0:KR, hl, T + 128 * qt:T + n], kst[ch][0:KR, hl, 0:n], start=True, stop=False))
                    ph.do("pe", lambda e, b: e.matmul(
                        pm[:, k, 128 * qt:n], identb[:, :], maskb[:, :], start=False, stop=True), f"mx{ch}")
                    reduce(ph, k, f"mx{ch}", mc[:, 8 * hl + 4 + qt:8 * hl + 5 + qt], pm[:, k, 0:n])
                return item

            for hl in range(8):
                out += [own(hl, qt) for qt in range(NQ)]
            for hl in range(8):
                for qt in range(NQ):
                    out += [cross(hl, qt, part) for part in range(3)]
                out.append(cross_rest(hl))

            def shift(ph):
                ph.wait("dve", "mx_part")
                ph.do("dve", lambda e, b: e.tensor_reduce(
                    mc[:, :].rearrange("p (h a q) -> p h a q", a=2, q=NQ)[:, :, 0, :], pmx[:, :, :, :],
                    AX.X, ALU.max), "mx_all")
                k = bank(ph, "act")
                ph.wait("pe", "mx_all")
                ph.do("pe", lambda e, b: e.transpose(pm[0:64, k, 0:128], mc[:, :], ident[:, :]), "mx_t",
                      alone=True)
                ph.wait("act", "mx_t", "mrow0", "mrow1")
                ph.do("act", lambda e, b: e.activation(mr[:, 0, :], pm[0:64, k, 0:128], ACT.Copy, scale=-1.0), "mr0")
                ph.wait("dve", "mr0", "mx_t", "mrow0", "mrow1")
                ph.do("dve", lambda e, b: e.scalar_tensor_tensor(
                    out=mr[:, 1, :], in0=pm[0:64, k, 0:128], scalar=-1.0, in1=mr[:, 0, :],
                    op0=ALU.mult, op1=ALU.subtract), "mr")
                freed(ph, k, "mr")
                ph.wait("sp", "mr", f"scores{ch}")
                for i in range(2):
                    ph.do("sp", lambda e, b, i=i: e.dma_start(
                        qst[ch][KR + i:KR + i + 1, :, :].rearrange("o t c -> o (t c)"),
                        mr[:, i, :]), f"mrow{ch}", sem=f"mrow{ch}", by=16)

            out.append(shift)
            return out

        slots = [(kind, v, kt) for v in range(2)
                 for kind, kt in [("cross", kt) for kt in range(NCT)] + [("self", kt) for kt in range(NQ)]]

        def shape_of(slot):
            kind, v, kt = slot
            if kind == "cross":
                return (128 if kt < NCT - 1 else REST), 0, kt, T + 128 * kt
            return 128, 128 * kt, NCT + kt, 128 * kt

        def scores(ph, ch, n, pair):
            kind, v, kt = slot = slots[n]
            m, q0, _, k0 = shape_of(slot)
            qc = 0 if kind == "cross" else T
            tt = 2 * v + pair
            ph.wait("pe", f"exp{pair}", f"mrow{ch}", f"q_{ch}", f"ck0_{ch}", f"ck3_{ch}")
            for p in range(2):
                ph.do("pe", lambda e, b, p=p: e.matmul(
                    ps[0:m, 2 * pair + p, q0:T], kst[ch][0:KR + 2, 4 * p + tt, k0:k0 + m],
                    qst[ch][0:KR + 2, 4 * p + tt, qc + q0:qc + T],
                    start=True, stop=True), f"scores{ch}" if p else None)
            ph.wait("act", f"scores{ch}", f"pv{n % 2}")
            ph.do("act", lambda e, b: e.activation(
                prob[0:m, n % 2, 2 * pair:2 * pair + 2, q0:T], ps[0:m, 2 * pair:2 * pair + 2, q0:T],
                ACT.Exp, scale=SCALE), f"exp{pair}")
            if pair == 1:
                ph.named[f"prob{n % 2}"] = ph.named["exp1"]
                if kind == "self":
                    ph.wait("pool", "exp1")
                    ph.do("pool", lambda e, b: e.affine_select(
                        out=prob[:, n % 2, :, q0:q0 + 128], in_=prob[:, n % 2, :, q0:q0 + 128],
                        compare_op=ALU.is_ge, fill=0.0, base=0, pattern=[[0, 4], [1, 128]],
                        channel_multiplier=-1), f"prob{n % 2}")

        def weighted(ph, ch, n):
            kind, v, kt = slot = slots[n]
            m, q0, vi, _ = shape_of(slot)
            g = 2 * ch + v
            last = kt == (NCT if kind == "cross" else NQ) - 1
            ph.wait("pe", f"prob{n % 2}", "vt")
            if kt == 0:
                ph.wait("pe", "outs")
            for j in range(4):
                hl = 4 * (j % 2) + 2 * v + j // 2
                ph.do("pe", lambda e, b, j=j, hl=hl: e.matmul(
                    po[32 * j:32 * j + 32, q0:T], vt[ch][0:m, vi, VE * hl:VE * hl + 32], prob[0:m, n % 2, j, q0:T],
                    start=kt == 0, stop=last), f"pv{n % 2}" if j == 3 else None)
            ph.named[f"values{ch}"] = ph.named[f"pv{n % 2}"]
            if not last:
                return None
            i = 0 if kind == "cross" else 1
            ph.wait("act", f"pv{n % 2}", "y_mul")
            ph.do("act", lambda e, b: e.copy(oc[:, i, :], po[:, :]), "outs")
            if i == 0:
                return None
            ph.wait("pool", "outs")
            ph.do("pool", lambda e, b: e.dma_start(
                scr["dn1"], bass.AP(oc[:, :, :].tensor, D * 2 * T, [[32 * 2 * T, 4], [1, 2 * T]])),
                "dn1", sem="dn1", by=16)
            ph.wait("pool", "dn1", "inv")
            ph.do("pool", lambda e, b: e.dma_start(
                dsum[:, :], scr["dn1"].rearrange("j (r c) -> (j r) c", c=32)), "dc", sem="dc", by=16)

            def divide(ph):
                ph.wait("dve", "dc")
                ph.do("dve", lambda e, b: e.reciprocal(dsum[:, :], dsum[:, :]), "inv")
                ph.wait("pool", "inv")
                ph.do("pool", lambda e, b: e.dma_start(
                    scr["dn2"].rearrange("j (r c) -> (j r) c", c=32), dsum[:, :]), "dn2", sem="dn2", by=16)
                ph.wait("pool", "dn2", "y_mul")
                for j in range(4):
                    ph.do("pool", lambda e, b, j=j: e.dma_start(
                        den[32 * j:32 * j + 32, :, :].rearrange("p a n -> p (a n)"),
                        scr["dn2"][j, :].partition_broadcast(32)), "den", sem="den", by=16)
                ph.wait("pool", "den")
                ph.do("pool", lambda e, b: e.tensor_tensor(oc[:, :, :], oc[:, :, :], den[:, :, :], ALU.mult), "y_mul")
                ph.wait("pool", "y_mul", "y_read")
                ph.do("pool", lambda e, b: e.tensor_tensor(yg[:, g, :], oc[:, 0, :], oc[:, 1, :], ALU.add), "y_sum")
                ph.named["y_mul"] = ph.named["y_sum"]
            return divide

        def finish_items(d):
            out = []
            rows = lambda dram, b: dram[bass.ds((b + d) * T, T), :].rearrange("(q p) c -> p q c", p=128)

            def start(ph):
                ph.wait("sp", "ct_read", "x1_out")
                ph.do("sp", lambda e, b: e.dma_start(xr[:, :, :], x[b + d].rearrange("(q p) c -> p q c", p=128)),
                      "xr", sem="xr", by=16)
                ph.wait("pool", "xr", "bpt")
                for q in range(NQ):
                    ph.do("pool", lambda e, b, q=q: e.tensor_tensor(xr[:, q, :], xr[:, q, :], bpt[:, :], ALU.add), "xrb")

            def outproj(q):
                def item(ph):
                    k = bank(ph, "dve")
                    ph.wait("pe", "y_sum")
                    for g in range(4):
                        ph.do("pe", lambda e, b, g=g: e.matmul(
                            pm[:, k, 0:C], yg[:, g, 128 * q:128 * q + 128], wp[:, g, :], start=g == 0, stop=g == 3),
                            "y_read" if g == 3 else None)
                    ph.wait("dve", "y_read", "xrb", "gates")
                    ph.do("dve", lambda e, b: e.scalar_tensor_tensor(
                        out=xr[:, q, :], in0=pm[:, k, 0:C], scalar=gates[:, 0:1], in1=xr[:, q, :],
                        op0=ALU.mult, op1=ALU.add), "x1")
                    freed(ph, k, "x1")
                    if q == NQ - 1:
                        row_stats(ph, xr, ("x1",))
                return item

            def norm2(ph):
                normalise(ph, xr, xa, "xn2")
                ph.wait("sp", "xn2")
                ph.do("sp", lambda e, b: e.dma_start(rows(scr["xn"], b), xa[:, :, :]),
                      "xn_out", sem="xn_out", by=16)

            def router(ph):
                k = bank(ph, "dve")
                ph.wait("pe", "xt")
                for q in range(NQ):
                    for kc in range(KC):
                        ph.do("pe", lambda e, b, q=q, kc=kc: e.matmul(
                            pm[:, k, E * q:E * q + E], xt[:, kc, 128 * q:128 * q + 128], wg[:, kc, :],
                            start=kc == 0, stop=kc == KC - 1), "xt_read" if q == NQ - 1 and kc == KC - 1 else None)
                ph.wait("dve", "xt_read", "lg_out")
                ph.do("dve", lambda e, b: e.tensor_copy(
                    lgt[:, :, :], pm[:, k, 0:E * NQ].rearrange("p (q e) -> p q e", e=E)), "lg")
                freed(ph, k, "lg")
                ph.wait("sp", "lg")
                ph.do("sp", lambda e, b: e.dma_start(rows(scr["lg"], b), lgt[:, :, :]), "lg_out", sem="lg_out", by=16)

            def hidden(m):
                def item(ph):
                    ka, kb = bank(ph, "dve"), bank(ph, "dve")
                    ph.wait("pe", "xt")
                    for k, wt in ((ka, ws1), (kb, ws3)):
                        for kc in range(KC):
                            ph.do("pe", lambda e, b, k=k, wt=wt, kc=kc: e.matmul(
                                pm[:, k, :], wt[:, kc, 128 * m:128 * m + 128], xt[:, kc, :],
                                start=kc == 0, stop=kc == KC - 1), "xt_read" if kc == KC - 1 else None)
                    ph.wait("act", "xt_read", "slot0", "slot1", "wr0", "wr1", "act_t")
                    ph.do("act", lambda e, b: e.activation(sig_t[:, 0, :], pm[:, ka, :], ACT.Tanh, scale=0.5), "tanh")
                    ph.wait("dve", "tanh")
                    ph.do("dve", lambda e, b: e.scalar_tensor_tensor(
                        out=sig_t[:, 1, :], in0=sig_t[:, 0, :], scalar=1.0, in1=pm[:, ka, :],
                        op0=ALU.add, op1=ALU.mult), "silu")
                    freed(ph, ka, "silu")
                    ph.wait("dve", "silu", "z_read")
                    ph.do("dve", lambda e, b: e.scalar_tensor_tensor(
                        out=act_t[:, m, :], in0=sig_t[:, 1, :], scalar=0.5, in1=pm[:, kb, :],
                        op0=ALU.mult, op1=ALU.mult), "act_t")
                    freed(ph, kb, "act_t")
                return item

            def shared_out(q):
                def item(ph):
                    k = bank(ph, "dve")
                    ph.wait("pe", "act_t")
                    for m in range(KC):
                        ph.do("pe", lambda e, b, m=m: e.matmul(
                            pm[:, k, 0:C], act_t[:, m, 128 * q:128 * q + 128], ws2[:, m, :],
                            start=m == 0, stop=m == KC - 1), "z_read" if m == KC - 1 else None)
                    ph.wait("dve", "z_read", "x1", "ln_a")
                    ph.do("dve", lambda e, b: e.scalar_tensor_tensor(
                        out=xr[:, q, :], in0=pm[:, k, 0:C], scalar=gates[:, 1:2], in1=xr[:, q, :],
                        op0=ALU.mult, op1=ALU.add), "x1z")
                    freed(ph, k, "x1z")
                    if q == NQ - 1:
                        ph.wait("sp", "x1z")
                        ph.do("sp", lambda e, b: e.dma_start(rows(scr["x1z"], b), xr[:, :, :]),
                              "x1_out", sem="x1_out", by=16)
                return item

            out.append(start)
            out += [outproj(q) for q in range(NQ)]
            out.append(norm2)
            out += [transpose_item(xa, "xn2", ("xt_read",), "xn2_t", kc) for kc in range(KC)]
            out.append(router)
            out += [hidden(m) for m in range(KC)]
            out += [shared_out(q) for q in range(NQ)]
            return out

        def stats1(ph):
            row_stats(ph, xa, ("x",))

        def norm1(ph):
            normalise(ph, xa, xa, "ln1")

        def first_items():
            return [transpose_item(xa, "ln1", ("xt_read",), "ln1_t", kc) for kc in range(KC)]

        def spread(items, lo, hi, table):
            for i, it in enumerate(items):
                table.setdefault(lo + i * (hi - lo) // max(1, len(items)), []).append(it)

        NS = len(slots)

        def half(ph, ch, table, pending):
            later = {}
            for n in range(NS):
                for fn in later.pop(n, []):
                    fn(ph)
                for pair in range(2):
                    scores(ph, ch, n, pair)
                    for it in table.get(2 * n + pair, []):
                        it(ph)
                if pending is not None:
                    div = weighted(ph, *pending)
                    if div:
                        later.setdefault(n + 3, []).append(div)
                pending = (ch, n)
            assert not later
            return pending

        def body(ph, first, last):
            t0, t1 = {}, {}
            operands, values = project_items(1)
            spread(operands, 1, 8, t0)
            spread(values, 9, 16, t0)
            if not first:
                fin = finish_items(-1)
                for at, it in zip((15, 18, 19, 20, 21, 24, 27, 28, 30, 32, 34, 38, 39, 40, 41), fin, strict=True):
                    t0.setdefault(at, []).append(it)
            spread(max_items(1), 18, 2 * NS - 5, t0)
            if not last:
                t0.setdefault(50, []).append(lambda ph: load_ctx(ph, 1))
                t0.setdefault(46, []).append(lambda ph: load_x(ph, 1))
                t0.setdefault(56, []).append(stats1)
                t0.setdefault(60, []).append(norm1)
                operands, values = project_items(0)
                spread(first_items(), 0, 1, t1)
                spread(operands, 2, 9, t1)
                spread(values, 10, 15, t1)
                spread(max_items(0), 18, 2 * NS - 5, t1)
            pend = half(ph, 0, t0, None if first else (1, NS - 1))
            half(ph, 1, t1, pend)

        P = Phase()
        load_weights(P)
        load_x(P, 0)
        load_ctx(P, 0)
        stats1(P)
        norm1(P)
        operands, values = project_items(0)
        for it in first_items() + operands + values + max_items(0):
            it(P)
        for e in ENGINES:
            P.wait(e, "w", "gates", "bpt", "identb", "mask", "c2", "vt_ones", "st_ones")
        for k in ("w", "gates", "bpt", "ident", "identb", "mask", "c0", "c1", "c2", "vt_ones", "st_ones"):
            P.named.pop(k)
        F = Phase(P)
        body(F, True, False)
        r0, p0 = ring.n, pieces[0]
        M0 = Phase(F)
        body(M0, False, False)
        assert (ring.n - r0) % 3 == 0 and (pieces[0] - p0) % 2 == 0, (ring.n - r0, pieces[0] - p0)
        M = Phase(M0)
        body(M, False, False)
        L = Phase(M)
        body(L, False, True)
        X = Phase(L)
        div = weighted(X, 1, NS - 1)
        div(X)
        for it in finish_items(0):
            it(X)
        X.wait("sp", "x1_out", "xn_out", "lg_out")

        assert B >= 3
        before_m = total(P, F)

        block = ctx.enter_context(nc.Block())

        def program(name):
            def emit(eng):
                P.run(name, eng, sems, {}, 0)
                F.run(name, eng, sems, total(P), 0)
                with eng.Fori(1, B - 1) as b:
                    base = {s: before_m.get(s, 0) + (b - 1) * M.count.get(s, 0) for s in names}
                    M.run(name, eng, sems, base, b)
                done = {s: before_m.get(s, 0) + (B - 2) * M.count.get(s, 0) for s in names}
                L.run(name, eng, sems, done, B - 1)
                done = {s: n + L.count.get(s, 0) for s, n in done.items()}
                X.run(name, eng, sems, done, B - 1)
            return emit

        block.tensor(program("pe"))
        block.scalar(program("act"))
        block.vector(program("dve"))
        block.gpsimd(program("pool"))
        block.sync(program("sp"))


def run_phases(nc, ctx, sems, first, body, last, count):
    block = ctx.enter_context(nc.Block())

    def program(name):
        def emit(eng):
            first.run(name, eng, sems, {}, 0)
            start = total(first)
            with eng.Fori(1, 1 + count) as i:
                base = {s: start.get(s, 0) + (i - 1) * body.count.get(s, 0) for s in sems}
                body.run(name, eng, sems, base, i)
            done = {s: start.get(s, 0) + count * body.count.get(s, 0) for s in sems}
            last.run(name, eng, sems, done, count + 1)
        return emit

    block.tensor(program("pe"))
    block.scalar(program("act"))
    block.vector(program("dve"))
    block.gpsimd(program("pool"))
    block.sync(program("sp"))


def limits(B):
    tokens = 512 * B
    pairs, E, GR = 4 * tokens, 32, 256
    cap = 4 * pairs // E
    stride = cap + GR
    groups = -(-((pairs + E * (GR - 1)) // GR) // 4) * 4
    dump = E * stride
    return tokens, cap, stride, groups, dump


def build_route(nc, B, w, scr):
    E, NQ, K = 32, 4, 4
    tokens, cap, stride, groups, dump = limits(B)
    with ExitStack() as ctx:
        def sb(name, shape, dt=F32):
            return ctx.enter_context(nc.sbuf_tensor(name, shape, dt))
        lg = [sb(f"r_lg{i}", [128, NQ, E]) for i in range(2)]
        xs = [sb(f"r_xs{i}", [128, NQ, 256]) for i in range(2)]
        s = sb("r_s", [128, NQ, E])
        t = sb("r_t", [128, NQ, E])
        hot = sb("r_hot", [128, K, NQ, E])
        pick = sb("r_pick", [128, K, NQ, E])
        mem = sb("r_mem", [128, NQ, E], BF16)
        place = sb("r_place", [128, NQ, E])
        small = sb("r_small", [128, 3, NQ])
        best = sb("r_best", [128, K, NQ])
        wt = sb("r_wt", [128, K, NQ])
        rowf = sb("r_rowf", [128, K, NQ])
        ok = sb("r_ok", [128, K, NQ])
        rows = [sb(f"r_rows{i}", [128, K, NQ], I32) for i in range(2)]
        wout = [sb(f"r_wout{i}", [128, K, NQ]) for i in range(2)]
        cnt = sb("r_cnt", [128, E])
        down = sb("r_down", [128, E])
        first_row = sb("r_first", [128, E])
        over = [sb(f"r_over{i}", [128, K, NQ]) for i in range(2)]
        tri = sb("r_tri", [128, 128], BF16)
        ones = sb("r_ones", [128, 128], BF16)
        gate = sb("r_gate", [128, 1])
        pr = ctx.enter_context(nc.psum_tensor("r_rank", [128, 512], F32))
        names = list(ENGINES) + ["rg", "rlg0", "rlg1", "rxs0", "rxs1", "rsc0", "rsc1", "rout0", "rout1", "rcnt"] + [f"spare_{e}" for e in ENGINES]
        sems = {n: ctx.enter_context(nc.semaphore(f"r_{n}")) for n in names}

        def consts(ph):
            ph.do("sp", lambda e, b: e.dma_start(gate[:, :], w["g_ffn"].partition_broadcast(128)), "g", sem="rg", by=16)
            ph.do("pool", lambda e, b: e.memset(tri[:, :], 1.0), "tri0")
            ph.wait("pool", "tri0")
            ph.do("pool", lambda e, b: e.affine_select(
                out=tri[:, :], in_=tri[:, :], compare_op=ALU.is_gt, fill=0.0, base=0,
                pattern=[[1, 128]], channel_multiplier=-1), "tri")
            ph.wait("pool", "tri")
            ph.do("pool", lambda e, b: e.iota(down[:, :], pattern=[[-1, E]], base=E, channel_multiplier=0,
                                              allow_small_or_imprecise_dtypes=True), "iota")
            ph.wait("pool", "iota")
            ph.do("pool", lambda e, b: e.iota(first_row[:, :], pattern=[[stride, E]], base=0, channel_multiplier=0,
                                              allow_small_or_imprecise_dtypes=True), "iota")
            ph.wait("pool", "iota")
            for i in range(2):
                ph.do("pool", lambda e, b, i=i: e.iota(
                    over[i][:, :, :].rearrange("p k q -> p (k q)"), pattern=[[128, K * NQ]], base=dump + 128 * K * NQ * i,
                    channel_multiplier=1, allow_small_or_imprecise_dtypes=True), "iota")
                ph.wait("pool", "iota")
            ph.do("dve", lambda e, b: e.memset(ones[:, :], 1.0), "ones")
            ph.do("dve", lambda e, b: e.memset(cnt[:, :], 0.0), "cnt")
            ph.wait("act", "g")
            ph.do("act", lambda e, b: e.activation(gate[:, :], gate[:, :], ACT.Tanh), "gate")

        def load(ph, d, i):
            view = lambda dram, b: dram[bass.ds((2 * b + d) * 512, 512), :].rearrange("(q p) c -> p q c", p=128)
            ph.wait("sp", f"lg_read{i}")
            ph.do("sp", lambda e, b: e.dma_start(lg[i][:, :, :], view(scr["lg"], b)), f"lg{i}", sem=f"rlg{i}", by=16)
            ph.wait("sp", f"sc{i}")
            ph.do("sp", lambda e, b: e.dma_start(xs[i][:, :, :], view(scr["xn"], b)), f"xs{i}", sem=f"rxs{i}", by=16)

        def route(ph, d, i):

            def dve(fn, name="step", *waits):
                ph.wait("dve", *waits, "step")
                ph.do("dve", fn, name)
                ph.named["step"] = ph.named[name]

            bc = lambda a: a.unsqueeze(2).broadcast_to([128, NQ, E])
            per = lambda a: a.unsqueeze(1).broadcast_to([128, NQ, E])
            dve(lambda e, b: e.tensor_reduce(small[:, 0, :], lg[i][:, :, :], AX.X, ALU.max), "step", f"lg{i}")
            dve(lambda e, b: e.tensor_tensor(s[:, :, :], lg[i][:, :, :], bc(small[:, 0, :]), ALU.subtract), f"lg_read{i}")
            ph.wait("act", f"lg_read{i}")
            ph.do("act", lambda e, b: e.activation(s[:, :, :], s[:, :, :], ACT.Exp), "exp")
            dve(lambda e, b: e.tensor_reduce(small[:, 1, :], s[:, :, :], AX.X, ALU.add), "step", "exp")
            dve(lambda e, b: e.reciprocal(small[:, 2, :], small[:, 1, :]))
            dve(lambda e, b: e.tensor_tensor(s[:, :, :], s[:, :, :], bc(small[:, 2, :]), ALU.mult))
            for k in range(K):
                dve(lambda e, b, k=k: e.tensor_reduce(wt[:, k, :], s[:, :, :], AX.X, ALU.max))
                dve(lambda e, b, k=k: e.tensor_tensor(t[:, :, :], s[:, :, :], bc(wt[:, k, :]), ALU.is_equal))
                dve(lambda e, b: e.tensor_tensor(t[:, :, :], t[:, :, :], per(down[:, :]), ALU.mult), "step", "iota")
                dve(lambda e, b, k=k: e.tensor_reduce(best[:, k, :], t[:, :, :], AX.X, ALU.max))
                dve(lambda e, b, k=k: e.tensor_tensor(hot[:, k, :, :], per(down[:, :]), bc(best[:, k, :]), ALU.is_equal))
                dve(lambda e, b, k=k: e.scalar_tensor_tensor(
                    out=s[:, :, :], in0=hot[:, k, :, :], scalar=-2.0, in1=s[:, :, :], op0=ALU.mult, op1=ALU.add))
            dve(lambda e, b: e.tensor_scalar(mem[:, :, :], s[:, :, :], 0.0, None, ALU.is_lt), "mem", "ranks")
            ph.wait("pe", "mem", "tri", "ones", "cnt")
            for q in range(NQ + 1):
                for p in range(min(q, NQ - 1) + 1):
                    mat = tri if p == q else ones
                    ph.do("pe", lambda e, b, q=q, p=p, mat=mat: e.matmul(
                        pr[:, E * q:E * q + E], mat[:, :], mem[:, p, :], start=p == 0, stop=p == min(q, NQ - 1)),
                        "ranks" if q == NQ and p == NQ - 1 else None)
            dve(lambda e, b: e.tensor_tensor(place[:, :, :], pr[:, 0:E * NQ].rearrange("p (q e) -> p q e", e=E),
                                             per(cnt[:, :]), ALU.add), "step", "ranks")
            dve(lambda e, b: e.tensor_tensor(cnt[:, :], cnt[:, :], pr[:, E * NQ:E * NQ + E], ALU.add), "cnt")
            dve(lambda e, b: e.tensor_tensor(pick[:, :, :, :].rearrange("p k q e -> p k (q e)"),
                                             hot[:, :, :, :].rearrange("p k q e -> p k (q e)"),
                                             place[:, :, :].rearrange("p q e -> p (q e)").unsqueeze(1).broadcast_to([128, K, NQ * E]),
                                             ALU.mult))
            dve(lambda e, b: e.tensor_reduce(ok[:, :, :], pick[:, :, :, :], AX.X, ALU.add))
            dve(lambda e, b: e.tensor_scalar(rowf[:, :, :], best[:, :, :], float(-stride), float(E * stride), ALU.mult, ALU.add))
            dve(lambda e, b: e.tensor_tensor(rowf[:, :, :], rowf[:, :, :], ok[:, :, :], ALU.add))
            dve(lambda e, b: e.tensor_scalar(ok[:, :, :], ok[:, :, :], float(cap), None, ALU.is_lt))
            dve(lambda e, b: e.tensor_tensor(rowf[:, :, :], rowf[:, :, :], over[i][:, :, :], ALU.subtract))
            dve(lambda e, b: e.tensor_tensor(rowf[:, :, :], rowf[:, :, :], ok[:, :, :], ALU.mult))
            dve(lambda e, b: e.tensor_tensor(rowf[:, :, :], rowf[:, :, :], over[i][:, :, :], ALU.add))
            dve(lambda e, b: e.tensor_copy(rows[i][:, :, :], rowf[:, :, :]), "rows", f"sc{i}", f"out{i}")
            dve(lambda e, b: e.tensor_scalar(wt[:, :, :], wt[:, :, :], gate[:, :], None, ALU.mult), "step", "gate")
            dve(lambda e, b: e.tensor_tensor(wout[i][:, :, :], wt[:, :, :], ok[:, :, :], ALU.mult), "wout")
            ph.wait("pool", "rows", f"xs{i}")
            for q in range(NQ):
                for k in range(K):
                    ph.do("pool", lambda e, b, q=q, k=k: e.indirect_dma_start(
                        scr["slots"], bass.IndirectOffsetOnAxis(ap=rows[i][:, k, q:q + 1].bitcast(U32), axis=0),
                        xs[i][:, q, :], None), f"sc{i}", sem=f"rsc{i}", by=16)
            ph.wait("sp", "rows", "wout")
            ph.do("sp", lambda e, b: e.dma_start(scr["rows"][bass.ds(2 * b + d, 1)].rearrange("o p c -> (o p) c"),
                                                 rows[i][:, :, :].rearrange("p k q -> p (k q)")), f"out{i}", sem=f"rout{i}", by=16)
            ph.do("sp", lambda e, b: e.dma_start(scr["wts"][bass.ds(2 * b + d, 1)].rearrange("o p c -> (o p) c"),
                                                 wout[i][:, :, :].rearrange("p k q -> p (k q)")), f"out{i}", sem=f"rout{i}", by=16)

        F = Phase()
        consts(F)
        load(F, 0, 0)
        load(F, 1, 1)
        for e in ENGINES:
            F.wait(e, "gate", "iota", "ones", "cnt", "tri")
        for k in ("gate", "iota", "ones", "tri", "g"):
            F.named.pop(k)

        def turn(ph, more):
            for i in range(2):
                route(ph, i, i)
                if more:
                    load(ph, i + 2, i)

        turn(F, True)
        M0 = Phase(F)
        turn(M0, True)
        M = Phase(M0)
        turn(M, True)
        X = Phase(M)
        turn(X, False)
        X.wait("sp", "cnt")
        X.do("sp", lambda e, b: e.dma_start(scr["cnt"], cnt[0:1, :]), "cnt_out", sem="rcnt", by=16)
        X.wait("sp", "sc0", "sc1", "cnt_out", "out0", "out1")
        run_phases(nc, ctx, sems, F, M, X, B // 2 - 2)


def build_experts(nc, B, w, scr):
    E, C, H, KC, GR = 32, 256, 128, 2, 256
    tokens, cap, stride, groups, dump = limits(B)
    U = 4
    with ExitStack() as ctx:
        def sb(name, shape, dt=F32):
            return ctx.enter_context(nc.sbuf_tensor(name, shape, dt))
        wall = sb("e_wall", [128, E, 2 * KC * H + C])
        we = [sb(f"e_we{i}", [128, 2 * KC * H + C]) for i in range(U)]
        ident = sb("e_ident", [128, 128])
        zero = sb("e_zero", [128, 2, C])
        xin = [sb(f"e_xin{i}", [128, 2, C]) for i in range(U)]
        xt = [sb(f"e_xt{i}", [128, KC, GR]) for i in range(2)]
        th = [sb(f"e_th{i}", [128, GR]) for i in range(2)]
        sl = [sb(f"e_sl{i}", [128, GR]) for i in range(2)]
        act = [sb(f"e_act{i}", [128, GR]) for i in range(2)]
        yo = [sb(f"e_yo{i}", [128, 2, C]) for i in range(2)]
        cnt = sb("e_cnt", [128, E])
        ncap = sb("e_ncap", [128, E])
        gend = sb("e_gend", [128, E])
        gtmp = sb("e_gtmp", [128, E])
        shift = sb("e_shift", [128, E])
        gint = sb("e_gint", [128, E], I32)
        firstz = sb("e_firstz", [128, E])
        zrow = sb("e_zrow", [128, E], I32)
        NC2 = -(-groups // 128)
        gid = sb("e_gid", [128, NC2])
        gcl = sb("e_gcl", [128, NC2])
        le = sb("e_le", [128, NC2, E])
        les = sb("e_les", [128, NC2, E])
        tab = sb("e_tab", [128, 2, NC2])
        tmp = sb("e_tmp", [128, 2, NC2])
        tabi = sb("e_tabi", [128, 2, NC2], I32)
        NT = NC2 * 128 + 4
        table = sb("e_table", [1, 2 * NT], I32)
        pt = [ctx.enter_context(nc.psum_tensor(f"e_pt{i}", [128, KC, GR], F32)) for i in range(2)]
        phd = [ctx.enter_context(nc.psum_tensor(f"e_ph{i}", [128, 2, GR], F32)) for i in range(2)]
        py = [ctx.enter_context(nc.psum_tensor(f"e_py{i}", [128, 2, C], F32)) for i in range(2)]
        names = list(ENGINES) + ["w", "cnt", "tab", "tab2", "zf"] + [f"xin{i}" for i in range(U)] + ["yo0", "yo1"] \
            + [f"spare_{e}" for e in ENGINES]
        sems = {n: ctx.enter_context(nc.semaphore(f"e_{n}")) for n in names}

        def tables(ph):
            ph.do("sp", lambda e, b: e.dma_start(cnt[:, :], scr["cnt"][0, :].partition_broadcast(128)), "cnt", sem="cnt", by=16)
            n0 = E // 4
            for i in range(4):
                es = slice(n0 * i, n0 * i + n0)
                for m, src in enumerate((w["W1"], w["W3"])):
                    for kc in range(KC):
                        ph.do("act", lambda e, b, m=m, src=src, es=es, kc=kc: e.dma_start(
                            wall[:, es, H * (KC * m + kc):H * (KC * m + kc) + H], src[es, 128 * kc:128 * kc + 128, :].rearrange("e p h -> p e h")), "w", sem="w", by=16)
                ph.do("act", lambda e, b, es=es: e.dma_start(wall[:, es, 2 * KC * H:], w["W2"][es].rearrange("e p c -> p e c")), "w", sem="w", by=16)

            def pool(fn, name="pstep"):
                ph.wait("pool", "pstep")
                ph.do("pool", fn, name)
                ph.named["pstep"] = ph.named[name]
            pool(lambda e, b: e.memset(ident[:, :], 0.0))
            pool(lambda e, b: e.affine_select(out=ident[:, :], in_=ident[:, :], compare_op=ALU.not_equal, fill=1.0,
                                              base=0, pattern=[[-1, 128]], channel_multiplier=1))
            pool(lambda e, b: e.iota(gid[:, :], pattern=[[128, NC2]], base=0, channel_multiplier=1,
                                     allow_small_or_imprecise_dtypes=True))
            pool(lambda e, b: e.iota(firstz[:, :], pattern=[[stride, E]], base=0, channel_multiplier=0,
                                     allow_small_or_imprecise_dtypes=True))
            ph.named["iotas"] = ph.named["pstep"]

            def dve(fn, *waits):
                ph.wait("dve", *waits, "step")
                ph.do("dve", fn, "step")
            dve(lambda e, b: e.memset(zero[:, :, :], 0.0))
            dve(lambda e, b: e.memset(table[:, :], 0))
            dve(lambda e, b: e.tensor_scalar(ncap[:, :], cnt[:, :], float(cap), None, ALU.min), "cnt")
            dve(lambda e, b: e.tensor_tensor(zrow[:, :], ncap[:, :], firstz[:, :], ALU.add), "iotas")
            ph.named["zrow"] = ph.named["step"]
            dve(lambda e, b: e.tensor_scalar(gint[:, :], ncap[:, :], float(GR - 1), None, ALU.add))
            dve(lambda e, b: e.tensor_scalar(gint[:, :], gint[:, :], 8, None, ALU.arith_shift_right))
            dve(lambda e, b: e.tensor_copy(gend[:, :], gint[:, :]))
            dve(lambda e, b: e.memset(shift[:, :], 0.0))
            dve(lambda e, b: e.tensor_scalar(shift[:, 1:E], gend[:, 0:E - 1], float(GR), float(-stride), ALU.mult, ALU.add))
            ph.named["shift"] = ph.named["step"]
            a, o = gend, gtmp
            n = 1
            while n < E:
                dve(lambda e, b, a=a, o=o, n=n: e.tensor_tensor(o[:, n:E], a[:, n:E], a[:, 0:E - n], ALU.add))
                dve(lambda e, b, a=a, o=o, n=n: e.tensor_copy(o[:, 0:n], a[:, 0:n]))
                a, o, n = o, a, 2 * n
            gsum = a
            last = gsum[:, E - 1:E]
            dve(lambda e, b: e.tensor_scalar(gcl[:, :], gid[:, :], 1.0, last, ALU.add, ALU.min))
            dve(lambda e, b: e.tensor_scalar(gcl[:, :], gcl[:, :], -1.0, None, ALU.add))
            bc = lambda v: v.unsqueeze(2).broadcast_to([128, NC2, E])
            per = lambda v: v.unsqueeze(1).broadcast_to([128, NC2, E])
            dve(lambda e, b: e.tensor_tensor(le[:, :, :], per(gsum[:, :]), bc(gcl[:, :]), ALU.is_le))
            dve(lambda e, b: e.tensor_tensor(les[:, :, :], le[:, :, :], per(gsum[:, :]), ALU.mult))
            dve(lambda e, b: e.tensor_reduce(tab[:, 0, :], le[:, :, :], AX.X, ALU.add))
            dve(lambda e, b: e.tensor_reduce(tmp[:, 0, :], les[:, :, :], AX.X, ALU.max))
            dve(lambda e, b: e.tensor_tensor(tmp[:, 0, :], gcl[:, :], tmp[:, 0, :], ALU.subtract))
            dve(lambda e, b: e.tensor_scalar(tmp[:, 0, :], tmp[:, 0, :], float(GR), None, ALU.mult))
            dve(lambda e, b: e.tensor_scalar(tmp[:, 1, :], tab[:, 0, :], float(stride), None, ALU.mult))
            dve(lambda e, b: e.tensor_tensor(tab[:, 1, :], tmp[:, 0, :], tmp[:, 1, :], ALU.add))
            dve(lambda e, b: e.tensor_copy(tabi[:, :, :], tab[:, :, :]))
            ph.named["tab"] = ph.named["step"]
            ph.wait("sp", "zrow")

            def fill(e, x):
                row = e.value_load(zrow[0:1, x:x + 1], min_val=0, max_val=dump - 1)
                return e.dma_start(scr["slots"][bass.ds(row, GR), :].rearrange("(q p) c -> p q c", p=128), zero[:, :, :])
            for x in range(E):
                ph.do("sp", lambda e, b, x=x: fill(e, x), "zf", sem="zf", by=16)
            ph.wait("sp", "shift", "tab")
            ph.do("sp", lambda e, b: e.dma_start(scr["shift"], shift[0:1, :]), "zf", sem="zf", by=16)
            ph.do("sp", lambda e, b: e.dma_start(scr["tab"].rearrange("k c p -> p k c"), tabi[:, :, :],
                                                 allow_slow_non_contiguous=True), "tab1", sem="tab", by=16)
            ph.wait("sp", "tab1")
            for k, at in ((0, 1), (1, NT)):
                ph.do("sp", lambda e, b, k=k, at=at: e.dma_start(
                    table[:, at:at + NC2 * 128], scr["tab"][k].rearrange("c p -> (c p)").unsqueeze(0)),
                    "table", sem="tab2", by=16)
            ph.wait("sp", "zf", "table")
            ph.wait("pe", "iotas")
            ph.wait("act", "w", "table")

        held = {}

        def entry(e, engine, k, b, d, hi):
            at = d + (1 if k == 0 else 0)
            if at % U == 0 or engine not in held:
                at -= at % U
                _, held[engine] = nc.values_load_multi_w_load_instructions(
                    table[0:1, bass.ds(U * b + at + k * NT, U)], engines=[engine], min_val=0, max_val=hi)
            return held[engine][(d + (1 if k == 0 else 0)) % U]

        def load(ph, u, d):
            ph.wait("sp", f"xr{u}")
            def go(e, b):
                row = entry(e, mybir.EngineType.SP, 1, b, d, dump - GR)
                return e.dma_start(xin[u][:, :, :], scr["slots"][bass.ds(row, GR), :].rearrange("(q p) c -> p q c", p=128))
            ph.do("sp", go, f"xin{u}", sem=f"xin{u}", by=16)

        def transposes(ph, u):
            i = u % 2
            ph.wait("pe", f"xin{u}", f"xt{i}")
            for kc in range(KC):
                for q in range(2):
                    ph.do("pe", lambda e, b, kc=kc, q=q: e.transpose(
                        pt[i][:, kc, 128 * q:128 * q + 128], xin[u][:, q, 128 * kc:128 * kc + 128], ident[:, :]),
                        f"xr{u}" if kc and q else None)
            ph.wait("act", f"xr{u}", f"h{i}")
            ph.do("act", lambda e, b: e.copy(xt[i][:, :, :], pt[i][:, :, :]), f"xt{i}")

        def weights(ph, u, d):
            ph.wait("act", f"y_of{u}")

            def go(e, b):
                x = entry(e, mybir.EngineType.Activation, 0, b, d, E - 1)
                return e.copy(we[u][:, :], wall[:, bass.ds(x, 1), :].rearrange("p o c -> p (o c)"))
            ph.do("act", go, f"we{u}")

        def hidden(ph, u, d):
            i = u % 2
            ph.wait("pe", f"xt{i}", f"we{u}", f"act{i}")
            for m in range(2):
                for kc in range(KC):
                    c0 = H * (KC * m + kc)
                    ph.do("pe", lambda e, b, m=m, kc=kc, c0=c0: e.matmul(
                        phd[i][:, m, :], we[u][:, c0:c0 + H], xt[i][:, kc, :], start=kc == 0, stop=kc == KC - 1),
                        f"h{i}" if m and kc == KC - 1 else None)
            ph.wait("act", f"h{i}", f"sl{i}")
            ph.do("act", lambda e, b: e.activation(th[i][:, :], phd[i][:, 0, :], ACT.Tanh, scale=0.5), f"th{i}")
            ph.wait("dve", f"th{i}", f"act{i}")
            ph.do("dve", lambda e, b: e.scalar_tensor_tensor(
                out=sl[i][:, :], in0=th[i][:, :], scalar=1.0, in1=phd[i][:, 0, :], op0=ALU.add, op1=ALU.mult), f"sl{i}")
            ph.wait("dve", f"sl{i}", f"y{i}")
            ph.do("dve", lambda e, b: e.scalar_tensor_tensor(
                out=act[i][:, :], in0=sl[i][:, :], scalar=0.5, in1=phd[i][:, 1, :], op0=ALU.mult, op1=ALU.mult), f"act{i}")

        def outs(ph, u, d):
            i = u % 2
            ph.wait("pe", f"act{i}", f"yc{i}")

            for q in range(2):
                ph.do("pe", lambda e, b, q=q: e.matmul(
                    py[i][:, q, :], act[i][:, 128 * q:128 * q + 128], we[u][:, 2 * KC * H:], start=True, stop=True),
                    f"y{i}" if q else None)
            ph.named[f"y_of{u}"] = ph.named[f"y{i}"]
            ph.wait("dve", f"y{i}", f"yo{i}")
            ph.do("dve", lambda e, b: e.tensor_copy(yo[i][:, :, :], py[i][:, :, :]), f"yc{i}")
            ph.wait("sp", f"yc{i}")

            ph.do("sp", lambda e, b: e.dma_start(
                scr["outs"][bass.ds((4 * b + d) * GR, GR), :].rearrange("(q p) c -> p q c", p=128), yo[i][:, :, :]),
                f"yo{i}", sem=f"yo{i}", by=16)

        def turn(ph, first, last):
            for u in range(U):
                hidden(ph, u, u)
                if not last or u < U - 1:
                    transposes(ph, (u + 1) % U)
                if not (first and u == 0):
                    outs(ph, (u - 1) % U, u - 1)
                if not last or u < U - 3:
                    weights(ph, (u + 3) % U, u + 3)
                if not last:
                    load(ph, u, u + U)

        F = Phase()
        tables(F)
        for u in range(U):
            load(F, u, u)
        for e in ENGINES:
            if e != "sp":
                F.wait(e, "table")
        for k in ("table", "w", "iotas", "zf"):
            F.named.pop(k)
        for u in range(3):
            weights(F, u, u)
        transposes(F, 0)
        turn(F, True, False)
        M0 = Phase(F)
        turn(M0, False, False)
        M = Phase(M0)
        turn(M, False, False)
        X = Phase(M)
        turn(X, False, True)
        outs(X, U - 1, U - 1)
        X.wait("sp", "yo0", "yo1")
        run_phases(nc, ctx, sems, F, M, X, groups // U - 2)


def build_combine(nc, B, w, scr, out):
    NQ, K, C = 4, 4, 256
    with ExitStack() as ctx:
        def sb(name, shape, dt=F32):
            return ctx.enter_context(nc.sbuf_tensor(name, shape, dt))
        E, GR = 32, 256
        tokens, cap, stride, groups, dump = limits(B)
        rows = [sb(f"c_rows{i}", [128, K * NQ], I32) for i in range(2)]
        gidx = [sb(f"c_gidx{i}", [128, K * NQ], I32) for i in range(2)]
        rowf = sb("c_rowf", [128, K * NQ])
        add_ = sb("c_add", [128, K * NQ])
        ge = sb("c_ge", [128, K * NQ, E])
        shift = sb("c_shift", [128, E])
        first_row = sb("c_first", [128, E])
        wt = [sb(f"c_wt{i}", [128, K * NQ]) for i in range(2)]
        acc = [sb(f"c_acc{i}", [128, NQ, C]) for i in range(2)]
        got = [sb(f"c_got{i}", [128, NQ, K, C]) for i in range(2)]
        names = list(ENGINES) + ["in0", "in1", "acc0", "acc1", "got0", "got1", "res0", "res1", "shift"] + [f"spare_{e}" for e in ENGINES]
        sems = {n: ctx.enter_context(nc.semaphore(f"c_{n}")) for n in names}
        view = lambda dram, b: dram[bass.ds(b * 512, 512), :].rearrange("(q p) c -> p q c", p=128)

        def load(ph, d, i):
            ph.wait("sp", f"idx{i}", f"sum{i}")
            ph.do("sp", lambda e, b: e.dma_start(rows[i][:, :], scr["rows"][bass.ds(2 * b + d, 1)].rearrange("o p c -> (o p) c")),
                  f"in{i}", sem=f"in{i}", by=16)
            ph.do("sp", lambda e, b: e.dma_start(wt[i][:, :], scr["wts"][bass.ds(2 * b + d, 1)].rearrange("o p c -> (o p) c")),
                  f"in{i}", sem=f"in{i}", by=16)
            ph.wait("sp", f"res{i}")
            ph.do("sp", lambda e, b: e.dma_start(acc[i][:, :, :], view(scr["x1z"], 2 * b + d)), f"acc{i}", sem=f"acc{i}", by=16)

        def gather(ph, i):
            ph.wait("dve", "step", f"in{i}")
            ph.do("dve", lambda e, b: e.tensor_copy(rowf[:, :], rows[i][:, :]), "step")
            ph.wait("dve", "step", "shift", "first")
            wide = [128, K * NQ, E]
            ph.do("dve", lambda e, b: e.tensor_tensor(
                ge[:, :, :], rowf[:, :].unsqueeze(2).broadcast_to(wide), first_row[:, :].unsqueeze(1).broadcast_to(wide),
                ALU.is_ge), "step")
            ph.wait("dve", "step")
            ph.do("dve", lambda e, b: e.tensor_tensor(
                ge[:, :, :], ge[:, :, :], shift[:, :].unsqueeze(1).broadcast_to(wide), ALU.mult), "step")
            ph.wait("dve", "step")
            ph.do("dve", lambda e, b: e.tensor_reduce(add_[:, :], ge[:, :, :], AX.X, ALU.add), "step")
            ph.wait("dve", "step")
            ph.do("dve", lambda e, b: e.tensor_tensor(rowf[:, :], rowf[:, :], add_[:, :], ALU.add), "step")
            ph.wait("dve", "step", f"got{i}")
            ph.do("dve", lambda e, b: e.tensor_scalar(
                gidx[i][:, :], rowf[:, :], float(GR * groups - 1), None, ALU.min), f"idx{i}")
            ph.named["step"] = ph.named[f"idx{i}"]
            ph.wait("pool", f"idx{i}", f"sum{i}")
            for q in range(NQ):
                for k in range(K):
                    ph.do("pool", lambda e, b, q=q, k=k: e.indirect_dma_start(
                        got[i][:, q, k, :], None, scr["outs"],
                        bass.IndirectOffsetOnAxis(ap=gidx[i][:, k * NQ + q:k * NQ + q + 1].bitcast(U32), axis=0)),
                        f"got{i}", sem=f"got{i}", by=16)

        def add(ph, d, i):
            ph.wait("dve", f"got{i}", f"acc{i}", f"in{i}")
            for k in range(K):
                for q in range(NQ):
                    ph.do("dve", lambda e, b, q=q, k=k: e.scalar_tensor_tensor(
                        out=acc[i][:, q, :], in0=got[i][:, q, k, :], scalar=wt[i][:, k * NQ + q:k * NQ + q + 1],
                        in1=acc[i][:, q, :], op0=ALU.mult, op1=ALU.add), f"sum{i}")
                if k < K - 1:
                    ph.wait("dve", f"sum{i}")
            ph.wait("sp", f"sum{i}")
            ph.do("sp", lambda e, b: e.dma_start(view(out, 2 * b + d), acc[i][:, :, :]), f"res{i}", sem=f"res{i}", by=16)

        F = Phase()
        load(F, 0, 0)
        load(F, 1, 1)
        F.do("sp", lambda e, b: e.dma_start(shift[:, :], scr["shift"][0, :].partition_broadcast(128)), "shift", sem="shift", by=16)
        F.do("pool", lambda e, b: e.iota(first_row[:, :], pattern=[[stride, E]], base=0, channel_multiplier=0,
                                         allow_small_or_imprecise_dtypes=True), "first")
        gather(F, 0)
        F.named.pop("shift")
        F.named.pop("first")

        def turn(ph, more):
            gather(ph, 1)
            add(ph, 0, 0)
            if more:
                load(ph, 2, 0)
                gather(ph, 0)
            add(ph, 1, 1)
            if more:
                load(ph, 3, 1)
        turn(F, True)
        M0 = Phase(F)
        turn(M0, True)
        M = Phase(M0)
        turn(M, True)
        X = Phase(M)
        turn(X, False)
        X.wait("sp", "res0", "res1")
        run_phases(nc, ctx, sems, F, M, X, B // 2 - 2)


def build(nc, arrays, out):
    x, ctx_t = arrays["x"], arrays["ctx_t"]
    B, T, C = x.shape
    w = {k.split("_")[-1]: a for k, a in arrays.items() if k.startswith("L0_")}
    w["g_xattn"], w["g_ffn"] = arrays["g_xattn"], arrays["g_ffn"]
    E = w["Wg"].shape[1]
    tokens, cap, stride, groups, dump = limits(B)

    def dram(name, shape, dt=F32):
        return nc.dram_tensor(f"scratch_{name}", shape, dt, kind="Internal").ap()

    scr = {
        "x1z": dram("x1z", [B * T, C]),
        "xn": dram("xn", [B * T, C]),
        "lg": dram("lg", [B * T, E]),
        "dn1": dram("dn1", [4, 2 * T]),
        "dn2": dram("dn2", [4, 2 * T]),
        "parts": dram("parts", [2, 3, 128, 1090], BF16),
        "slots": dram("slots", [dump + 2 * 128 * 16, C]),
        "outs": dram("outs", [256 * groups, C]),
        "rows": dram("rows", [B, 128, 16], I32),
        "wts": dram("wts", [B, 128, 16]),
        "cnt": dram("cnt", [1, E]),
        "shift": dram("shift", [1, E]),
        "tab": dram("tab", [2, -(-groups // 128), 128], I32),
    }
    build_attention(nc, B, x, ctx_t, w, scr)
    build_route(nc, B, w, scr)
    build_experts(nc, B, w, scr)
    build_combine(nc, B, w, scr, out)


def kernel(**inputs):
    import concourse.bacc as bacc
    from concourse.bass_utils import run_bass_kernel_spmd

    nc = bacc.Bacc("TRN2", target_bir_lowering=False, num_devices=1)
    data, args = {}, {}
    for name, value in inputs.items():
        value = np.asarray(value)
        if name == "ctx_512":
            name, value = "ctx_t", value.transpose(0, 2, 1)
        data[f"in_{name}_dram"] = np.ascontiguousarray(value)
        args[name] = nc.dram_tensor(f"in_{name}_dram", value.shape, F32, kind="ExternalInput").ap()
    shape = inputs["x"].shape
    out = nc.dram_tensor("out_0_dram", (shape[0] * shape[1], shape[2]), F32, kind="ExternalOutput").ap()
    build(nc, args, out)
    nc.compile()
    result = run_bass_kernel_spmd(nc, [data], core_ids=[0])
    return result.results[0]["out_0_dram"].reshape(shape)
```

```python
from contextlib import ExitStack

import numpy as np

import concourse.bass as bass
from concourse import mybir

F32 = mybir.dt.float32
BF16 = mybir.dt.bfloat16
I32 = mybir.dt.int32
U32 = mybir.dt.uint32
ALU = mybir.AluOpType
ACT = mybir.ActivationFunctionType
AX = mybir.AxisListType

ENGINES = ("pe", "act", "dve", "pool", "sp")


class Phase:

    def __init__(self, before=None):
        self.steps = {e: [] for e in ENGINES}
        self.count = {}
        self.waited = {}
        self.named = {}
        if before is not None:
            self.named = {k: (s, v - before.count.get(s, 0)) for k, (s, v) in before.named.items()}

    def do(self, engine, fn, name=None, sem=None, by=1, alone=False):
        sem = sem or engine
        if name is not None:
            self.count[sem] = self.count.get(sem, 0) + by
            self.named[name] = (sem, self.count[sem])
        self.steps[engine].append(("do", fn, sem if name is not None else None, by, alone or engine in ("pool", "sp")))

    def wait(self, engine, *names):
        for name in names:
            if name not in self.named:
                continue
            sem, value = self.named[name]
            if self.waited.get((engine, sem), -10**9) >= value:
                continue
            self.waited[(engine, sem)] = value
            self.steps[engine].append(("wait", sem, value))

    def run(self, engine, eng, sems, base, batch):
        pending = False
        for step in self.steps[engine]:
            if step[0] == "wait":
                value = base.get(step[1], 0) + step[2]
                if isinstance(value, int) and value <= 0:
                    continue
                eng.wait_ge(sems[step[1]], value)
                pending = not isinstance(value, int)
                if pending and engine == "sp":
                    eng.sem_inc(sems["spare_sp"], 1)
                    pending = False
            else:
                if pending and step[4]:
                    eng.sem_inc(sems["spare_" + engine], 1)
                pending = False
                ins = step[1](eng, batch)
                if step[2] is not None:
                    ins.then_inc(sems[step[2]], step[3])


def total(*phases):
    out = {}
    for ph in phases:
        for s, n in ph.count.items():
            out[s] = out.get(s, 0) + n
    return out


def limits(B):
    tokens = 512 * B
    pairs, E, GR = 4 * tokens, 32, 256
    cap = 4 * pairs // E
    stride = cap + GR
    groups = -(-((pairs + E * (GR - 1)) // GR) // 4) * 4
    dump = E * stride
    return tokens, cap, stride, groups, dump


def load_experts(ph, wall, w, i):
    E, C, H = w["W1"].shape
    es = slice(E // 4 * i, E // 4 * (i + 1))
    parts = [(w[name][es, 128 * kc:128 * kc + 128, :], H) for name in ("W1", "W3") for kc in range(C // 128)]
    at = 0
    for src, n in parts + [(w["W2"][es], C)]:
        ph.do("act", lambda e, b, src=src, n=n, at=at: e.dma_start(
            wall[:, es, at:at + n], src.rearrange("e p c -> p e c")), "wall", sem="wall", by=16)
        at += n


def build_attention(nc, B, x, ctx_t, w, scr, stacks, wall):
    T, C, TC, CC, H, D = 512, 256, 1601, 128, 16, 16
    E, K = w["Wg"].shape[1], 4
    tokens, cap, stride, groups, dump = limits(B)
    NQ = T // 128
    KC = C // 128
    NCT = (TC + 127) // 128
    REST = TC - 128 * (NCT - 1)
    VE = D + 1
    VW = 8 * VE
    QP, KP = (0, 0, 1, 1, 0, 2), (0, 1, 0, 1, 2, 0)
    KR = D * len(QP)
    SCALE = 1.0 / float(np.sqrt(D))
    EPS = 1e-5

    with ExitStack() as ctx:
        def sb(name, shape, dt=F32):
            return ctx.enter_context(nc.sbuf_tensor(name, shape, dt))

        wq = sb("wq", [128, KC, C])
        wk = sb("wk", [128, KC, C])
        wv = sb("wv", [128, KC, C])
        wcq = sb("wcq", [128, KC, C])
        wck = sb("wck", [128, C])
        wcv = sb("wcv", [128, C])
        wp = sb("wp", [128, 4, C])
        wg = sb("wg", [128, KC, E])
        ws1 = sb("ws1", [128, KC, C])
        ws3 = sb("ws3", [128, KC, C])
        ws2 = sb("ws2", [128, KC, C])
        bcol = sb("bcol", [128, 4, 2])
        bvb = sb("bvb", [128, C])
        bcvb = sb("bcvb", [128, C])
        bpt = sb("bpt", [128, C])
        gates = sb("gates", [128, 2])
        ident = sb("ident", [128, 128])
        identb = sb("identb", [128, 128], BF16)
        maskb = sb("maskb", [128, 128], BF16)
        QW, KW = 8 * 2 * T, 8 * (T + TC + 1)
        cut = lambda at, n: stacks[:, at:at + n].rearrange("p (h c) -> p h c", h=8)
        qst = [cut(QW * c, QW) for c in range(2)]
        kst = [cut(2 * QW + KW * c, KW) for c in range(2)]
        vt = [sb(f"vt{c}", [128, (NCT + NQ) * VW + 16]) for c in range(2)]
        SW = T + TC - 2 * 512 + 1
        split = [sb(f"split{i}", [128, 3 * SW], BF16) for i in range(2)]
        rest = sb("rest", [128, 2, 512])
        prob = sb("prob", [128, 2, 4, 512])
        xa = sb("xa", [128, NQ, C])
        xt = sb("xt", [128, KC, T])
        ct = sb("ct", [128, TC])
        yg = sb("yg", [128, 4, T])
        oc = sb("oc", [128, 2, T])
        dsum = sb("dsum", [128, 32])
        den = sb("den", [128, 2, T])
        stat = sb("stat", [128, NQ, 6])
        mv = sb("mv", [128, NQ, 2])
        rstd = sb("rstd", [128, NQ])
        var = sb("var", [128, NQ])
        newt = sb("newt", [128, NQ])
        lgt = sb("lgt", [128, NQ, E])
        pmx = sb("pmx", [128, 8, NQ, 4])
        mc = sb("mc", [128, 64])
        mr = sb("mr", [64, 2, 128], BF16)
        SB, RB = 3, 4
        ps = ctx.enter_context(nc.psum_tensor("scores", [128, SB, 512], F32))
        pm = ctx.enter_context(nc.psum_tensor("ring", [128, RB, 512], F32))
        po = ctx.enter_context(nc.psum_tensor("outs", [128, 512], F32))
        xr = ct[:, 0:NQ * C].rearrange("p (q c) -> p q c", c=C)
        cnt = sb("cnt", [128, E])
        down = sb("down", [128, E])
        over = sb("over", [128, K * NQ])
        rows = sb("rows", [128, K * NQ], I32)
        wout = sb("wout", [128, K * NQ])
        tri = sb("tri", [128, 128], BF16)
        ones = sb("ones", [128, 128], BF16)
        xs = split[0][:, 0:4 * T].bitcast(F32)
        room = split[1][:, :].bitcast(F32)
        at = [0]

        def piece_of(n):
            at[0] += n
            return room[:, at[0] - n:at[0]]

        hot = piece_of(K * NQ * E)
        pick = piece_of(K * NQ * E)
        sm, eq, place = (piece_of(NQ * E) for _ in range(3))
        best, wt, rowf, ok = (piece_of(K * NQ) for _ in range(4))
        tot = piece_of(3 * NQ)
        mem = piece_of(NQ * E // 2).bitcast(BF16)
        act_t, sig_t = (s[:, 0:4 * T].bitcast(F32).rearrange("p (m n) -> p m n", m=2) for s in split)

        names = list(ENGINES) + ["w", "x", "xr", "ctx", "st_q", "st_ck0", "st_ck3", "wr0", "wr1", "mrow0", "mrow1",
                                 "dn1", "dc", "dn2", "den", "xn_out", "x1_out", "xs", "sc", "rows_out", "cnt_out", "wall"]
        names += [f"spare_{e}" for e in ENGINES]
        sems = {n: ctx.enter_context(nc.semaphore(f"s_{n}")) for n in names}

        class Ring:
            n = 0

        ring, score_ring = Ring(), Ring()
        held = set()
        kept = Ring()

        def keep(ph, name):
            kept.n += 1
            ph.named[f"kept{kept.n}"] = ph.named[name]
            return f"kept{kept.n}"

        def run_all(ph, items):
            for it in items:
                second = it(ph)
                if second is not None:
                    second(ph)

        def bank(ph, free):
            k = ring.n % RB
            ring.n += 1
            assert k not in held, "its reader isn't queued yet"
            held.add(k)
            ph.wait("pe", f"ring{k}")
            return k

        def freed(ph, k, name):
            held.discard(k)
            ph.named[f"ring{k}"] = ph.named[name]

        def load_weights(ph):
            def ld(dst, src, **kw):
                ph.do("sp", lambda e, b: e.dma_start(dst, src, **kw), "w", sem="w", by=16)
            for dst, src in ((wq, w["Wq"]), (wk, w["Wk"]), (wv, w["Wv"]), (wcq, w["Wcq"]),
                             (ws1, w["Ws1"]), (ws3, w["Ws3"]), (ws2, w["Ws2"]), (wg, w["Wg"])):
                ld(dst[:, :, :], src.rearrange("(k p) n -> p k n", p=128))
            ld(wck[:, :], w["Wck"])
            ld(wcv[:, :], w["Wcv"])
            for i, n in enumerate(("bq", "bk", "bcq", "bck")):
                ld(bcol[:, i, :], w[n].rearrange("(c p) -> p c", p=128), allow_slow_non_contiguous=True)
            ld(bvb[:, :], w["bv"].partition_broadcast(128))
            ld(bcvb[:, :], w["bcv"].partition_broadcast(128))
            ld(bpt[:, :], w["bp"].partition_broadcast(128))
            ld(gates[:, 0:1], w["g_xattn"].partition_broadcast(128))
            ld(gates[:, 1:2], w["g_ffn"].partition_broadcast(128))
            ph.do("pool", lambda e, b: e.memset(ident[:, :], 0.0), "c0")
            ph.do("pool", lambda e, b: e.memset(maskb[:, :], 0.0), "c1")
            ph.do("pool", lambda e, b: e.memset(wp[:, :, :], 0.0), "c2")
            ph.wait("pool", "c0", "c1")
            ph.do("pool", lambda e, b: e.affine_select(
                out=ident[:, :], in_=ident[:, :], compare_op=ALU.not_equal, fill=1.0, base=0,
                pattern=[[-1, 128]], channel_multiplier=1), "ident")
            ph.do("pool", lambda e, b: e.affine_select(
                out=maskb[:, :], in_=maskb[:, :], compare_op=ALU.is_ge, fill=-1e30, base=0,
                pattern=[[-1, 128]], channel_multiplier=1), "mask")
            ph.wait("pool", "ident")
            ph.do("pool", lambda e, b: e.tensor_copy(identb[:, :], ident[:, :]), "identb")
            ph.wait("pool", "identb")
            for fn in (
                lambda e, b: e.memset(tri[:, :], 1.0),
                lambda e, b: e.affine_select(out=tri[:, :], in_=tri[:, :], compare_op=ALU.is_gt, fill=0.0, base=0,
                                             pattern=[[1, 128]], channel_multiplier=-1),
                lambda e, b: e.memset(ones[:, :], 1.0),
                lambda e, b: e.memset(cnt[:, :], 0.0),
                lambda e, b: e.iota(down[:, :], pattern=[[-1, E]], base=E, channel_multiplier=0,
                                    allow_small_or_imprecise_dtypes=True),
                lambda e, b: e.iota(over[:, :], pattern=[[128, K * NQ]], base=dump, channel_multiplier=1,
                                    allow_small_or_imprecise_dtypes=True),
            ):
                ph.do("pool", fn, "rc")
                ph.wait("pool", "rc")
            for c in range(2):
                ph.do("dve", lambda e, b, c=c: e.memset(vt[c][:, :], 1.0), "vt_ones")
                ph.do("pool", lambda e, b, c=c: e.memset(kst[c][96:128, :, :], 1.0), "st_ones")
                ph.wait("pool", "st_ones")
            ph.wait("sp", "c2")
            for ch in range(2):
                for v in range(2):
                    for j in range(4):
                        h = ch * 8 + 4 * (j % 2) + 2 * v + j // 2
                        ph.do("sp", lambda e, b, g=2 * ch + v, j=j, h=h: e.dma_start(
                            wp[32 * j:32 * j + D, g, :], w["Wp"][h * D:(h + 1) * D, :]), "w", sem="w", by=16)
            ph.wait("act", "w")
            ph.do("act", lambda e, b: e.activation(gates[:, :], gates[:, :], ACT.Tanh), "gates")
            ph.wait("dve", "w", "gates")
            ph.do("dve", lambda e, b: e.tensor_scalar(bpt[:, :], bpt[:, :], gates[:, 0:1], None, ALU.mult), "bpt")
            ph.wait("pe", "w", "identb", "mask")

        def load_x(ph, d):
            ph.wait("sp", "xn2_t", "xn_out", "ln1_t")
            ph.do("sp", lambda e, b: e.dma_start(xa[:, :, :], x[b + d].rearrange("(q p) c -> p q c", p=128)),
                  "x", sem="x", by=16)

        def load_ctx(ph, d):
            ph.wait("sp", "ct_read", "x1_out")
            ph.do("sp", lambda e, b: e.dma_start(ct[:, :], ctx_t[b + d][:, 0:TC]), "ctx", sem="ctx", by=16)

        def row_stats(ph, src, got):
            ph.wait("dve", *got)
            for q in range(NQ):
                ph.do("dve", lambda e, b, q=q: e.bn_stats(stat[:, q, :], src[:, q, :]), "ln_a")
            ph.wait("dve", "ln_a")
            for q in range(NQ):
                ph.do("dve", lambda e, b, q=q: e.bn_aggr(mv[:, q, :], stat[:, q, :]), "ln_b", alone=True)
            ph.wait("dve", "ln_b")
            ph.do("dve", lambda e, b: e.tensor_scalar(var[:, :], mv[:, :, 1], EPS, None, ALU.add), "ln_c")
            ph.wait("dve", "ln_c", "rstd")
            ph.do("dve", lambda e, b: e.tensor_scalar(
                rstd[:, :].bitcast(I32), var[:, :].bitcast(I32), -0.5, float(0x5F3759DF), ALU.mult, ALU.add), "guess")
            ph.wait("pool", "guess")
            for _ in range(4):
                ph.do("pool", lambda e, b: e.tensor_tensor(newt[:, :], rstd[:, :], rstd[:, :], ALU.mult), "newt")
                ph.wait("pool", "newt")
                ph.do("pool", lambda e, b: e.tensor_tensor(newt[:, :], newt[:, :], var[:, :], ALU.mult), "newt")
                ph.wait("pool", "newt")
                ph.do("pool", lambda e, b: e.tensor_scalar(newt[:, :], newt[:, :], -0.5, 1.5, ALU.mult, ALU.add), "newt")
                ph.wait("pool", "newt")
                ph.do("pool", lambda e, b: e.tensor_tensor(rstd[:, :], rstd[:, :], newt[:, :], ALU.mult), "rstd")
                ph.wait("pool", "rstd")

        def normalise(ph, src, dst, out):
            ph.wait("dve", "rstd")
            for q in range(NQ):
                ph.do("dve", lambda e, b, q=q: e.tensor_scalar(
                    dst[:, q, :], src[:, q, :], mv[:, q, 0:1], rstd[:, q:q + 1], ALU.subtract, ALU.mult), out)

        def transpose_item(src, ready, readers, done, kc):
            def item(ph):
                k = bank(ph, "act")
                ph.wait("pe", ready)
                for q in range(NQ):
                    ph.do("pe", lambda e, b, q=q: e.transpose(
                        pm[:, k, 128 * q:128 * q + 128], src[:, q, 128 * kc:128 * kc + 128], ident[:, :]),
                        done if q == NQ - 1 else None)
                ph.wait("act", done, *readers)
                ph.do("act", lambda e, b: e.copy(xt[:, kc, :], pm[:, k, :]), "xt")
                freed(ph, k, "xt")
            return item

        pieces = [0]
        parts = [0]

        def split_item(ch, kind):
            i, wt, n0, n, at = {
                "cq": (2, wcq, 0, T, 0), "q": (0, wq, 0, T, T),
                "k": (1, wk, 0, T, 0), "ck0": (3, wck, 0, 512, T),
                "ck1": (3, wck, 512, 512, 0), "ck2": (3, wck, 1024, 512, 512), "ck3": (3, wck, 1536, TC - 1536, 1024)}[kind]
            first = kind in ("cq", "k", "ck1")
            cn = {"q": 2 * T, "ck0": 2 * T, "ck3": T + TC - 2 * T}.get(kind)

            def item(ph):
                k = bank(ph, "dve")
                if first:
                    pieces[0] += 1
                s = pieces[0] % 2
                cs = slice(128 * ch, 128 * ch + 128)
                if i == 3:
                    ph.wait("pe", "ctx")
                    ph.do("pe", lambda e, b: e.matmul(pm[:, k, 0:n], wck[:, cs], ct[:, n0:n0 + n],
                                                      start=True, stop=True), "ct_read")
                    done = "ct_read"
                else:
                    ph.wait("pe", "xt")
                    for kc in range(KC):
                        ph.do("pe", lambda e, b, kc=kc: e.matmul(pm[:, k, 0:n], wt[:, kc, cs], xt[:, kc, :],
                                                                 start=kc == 0, stop=kc == KC - 1),
                              "xt_read" if kc == KC - 1 else None)
                    done = "xt_read"
                bias = bcol[:, i, ch:ch + 1]
                part = [split[s][:, r * SW + at:r * SW + at + n] for r in range(3)]
                ri = parts[0] % 2
                parts[0] += 1
                ph.wait("act", done, f"wr{s}", "z_read", "sc", "routed")
                ph.do("act", lambda e, b: e.activation(part[0], pm[:, k, 0:n], ACT.Identity, bias=bias), "part0")
                got = keep(ph, "part0")

                def second(ph):
                    ph.wait("dve", got, f"part2_{ri}")
                    ph.do("dve", lambda e, b: e.scalar_tensor_tensor(
                        out=rest[:, ri, 0:n], in0=pm[:, k, 0:n], scalar=bias, in1=part[0],
                        op0=ALU.add, op1=ALU.subtract), "rest")
                    freed(ph, k, "rest")
                    ph.wait("dve", "rest", f"wr{s}", "z_read", "sc", "ranks")
                    ph.do("dve", lambda e, b: e.tensor_copy(part[1], rest[:, ri, 0:n]), "part1")
                    ph.wait("pool", "part1", "sc")
                    ph.do("pool", lambda e, b: e.tensor_tensor(part[2], rest[:, ri, 0:n], part[1], ALU.subtract),
                          f"part2_{ri}")
                    ph.named["part2"] = ph.named[f"part2_{ri}"]
                    if cn is None:
                        return
                    ph.wait("sp", "part2", f"st_{kind}")
                    ph.do("sp", lambda e, b: e.dma_start(
                        scr["parts"][PIECES.index(kind)][:, :, 0:cn].rearrange("k p c -> p k c"),
                        split[s][:, :].rearrange("p (k c) -> p k c", k=3)[:, :, 0:cn]), f"wr_{kind}", sem=f"wr{s}", by=16)
                    ph.named[f"wr{s}"] = ph.named[f"wr_{kind}"]
                return second
            return item

        PIECES = ("q", "ck0", "ck3")

        def stack_item(ch):
            def item(ph):
                ph.wait("sp", f"scores{ch}", f"mx{ch}", "st_ones")
                for kind, dst, c0, cn in (("q", qst, 0, 2 * T), ("ck0", kst, 0, 2 * T), ("ck3", kst, 2 * T, T + TC - 2 * T)):
                    ph.wait("sp", f"wr_{kind}", f"st_{kind}")
                    for r, src in enumerate(KP if dst is kst else QP):
                        ph.do("sp", lambda e, b, r=r, src=src, kind=kind, dst=dst, c0=c0, cn=cn: e.dma_start(
                            dst[ch][D * r:D * r + D, :, c0:c0 + cn],
                            scr["parts"][PIECES.index(kind)][src][:, 0:cn].rearrange("(h d) c -> d h c", d=D)),
                            f"st_{kind}", sem=f"st_{kind}", by=16)
                    ph.named[f"{kind}_{ch}"] = ph.named[f"st_{kind}"]
            return item

        def value_item(ch, k0, nk):
            def item(ph):
                k = bank(ph, "dve")
                cs = slice(128 * ch, 128 * ch + 128)
                rows = 128
                if k0 >= NCT:
                    ph.wait("pe", "xt")
                    for q in range(NQ):
                        for kc in range(KC):
                            ph.do("pe", lambda e, b, q=q, kc=kc: e.matmul(
                                pm[:, k, 128 * q:128 * q + 128], xt[:, kc, 128 * q:128 * q + 128], wv[:, kc, cs],
                                start=kc == 0, stop=kc == KC - 1), "xt_read" if q == NQ - 1 and kc == KC - 1 else None)
                    done, bb = "xt_read", bvb
                else:
                    ph.wait("pe", "ctx")
                    for i in range(nk):
                        r0 = 128 * (k0 + i)
                        rows = min(128, TC - r0)
                        ph.do("pe", lambda e, b, i=i, r0=r0, rows=rows: e.matmul(
                            pm[0:rows, k, 128 * i:128 * i + 128], ct[:, r0:r0 + rows], wcv[:, cs],
                            start=True, stop=True), "ct_read" if i == nk - 1 else None)
                    done, bb = "ct_read", bcvb
                got = keep(ph, done)

                def second(ph):
                    ph.wait("dve", got, f"values{ch}", "w", "vt_ones")
                    for i in range(nk):
                        ph.do("dve", lambda e, b, i=i: e.tensor_tensor(
                            vt[ch][0:rows, VW * (k0 + i):VW * (k0 + i + 1)].rearrange("p (h e) -> p h e", e=VE)[:, :, 0:D],
                            pm[0:rows, k, 128 * i:128 * i + 128].rearrange("p (h d) -> p h d", d=D),
                            bb[0:rows, cs].rearrange("p (h d) -> p h d", d=D), ALU.add), "vt")
                    freed(ph, k, "vt")
                return second
            return item

        def project_items(ch):
            v = [value_item(ch, 4 * i, min(4, NCT - 4 * i)) for i in range(4)]
            p = {k: split_item(ch, k) for k in ("cq", "q", "k", "ck0", "ck1", "ck2", "ck3")}
            return [p["cq"], p["q"], p["k"], p["ck0"], p["ck1"], p["ck2"], p["ck3"]], v + [value_item(ch, NCT, NQ)]

        def max_items(ch):
            out, costs = [], []

            def reduce(ph, k, done, dst, src, name="mx_part"):
                ph.wait("dve", done)
                ph.do("dve", lambda e, b: e.tensor_reduce(dst, src, AX.X, ALU.max), name)
                freed(ph, k, name)

            def cross(hl, qt, part):
                def item(ph):
                    k = bank(ph, "dve")
                    ph.wait("pe", f"q_{ch}", f"ck0_{ch}", f"ck3_{ch}")
                    ph.do("pe", lambda e, b: e.matmul(
                        pm[:, k, :], qst[ch][0:KR, hl, 128 * qt:128 * qt + 128],
                        kst[ch][0:KR, hl, T + 512 * part:T + 512 * part + 512], start=True, stop=True), f"mx{ch}")
                    reduce(ph, k, f"mx{ch}", pmx[:, hl, qt, part:part + 1], pm[:, k, :])
                return item

            def cross_rest(hl):
                def item(ph):
                    k = bank(ph, "dve")
                    ph.wait("pe", f"q_{ch}", f"ck0_{ch}", f"ck3_{ch}")
                    for qt in range(NQ):
                        ph.do("pe", lambda e, b, qt=qt: e.matmul(
                            pm[:, k, 66 * qt:66 * qt + 66], qst[ch][0:KR, hl, 128 * qt:128 * qt + 128],
                            kst[ch][0:KR, hl, T + TC - 66:T + TC], start=True, stop=True), f"mx{ch}" if qt == NQ - 1 else None)
                    reduce(ph, k, f"mx{ch}", pmx[:, hl, :, 3], pm[:, k, 0:66 * NQ].rearrange("p (q n) -> p q n", q=NQ))
                return item

            def own(hl, qt):
                def item(ph):
                    k = bank(ph, "dve")
                    n = 128 * (qt + 1)
                    ph.wait("pe", f"q_{ch}", f"ck0_{ch}")
                    ph.do("pe", lambda e, b: e.matmul(
                        pm[:, k, 0:n], qst[ch][0:KR, hl, T + 128 * qt:T + n], kst[ch][0:KR, hl, 0:n], start=True, stop=False))
                    ph.do("pe", lambda e, b: e.matmul(
                        pm[:, k, 128 * qt:n], identb[:, :], maskb[:, :], start=False, stop=True), f"mx{ch}")
                    reduce(ph, k, f"mx{ch}", mc[:, 8 * hl + 4 + qt:8 * hl + 5 + qt], pm[:, k, 0:n])
                return item

            for hl in range(8):
                out += [own(hl, qt) for qt in range(NQ)]
                costs += [0.35 + 0.18 * qt for qt in range(NQ)]
            for hl in range(8):
                for qt in range(NQ):
                    out += [cross(hl, qt, part) for part in range(3)]
                out.append(cross_rest(hl))
                costs += [0.82] * (3 * NQ) + [0.46]
            return out, costs

        def shift_items(ch):
            def whole(ph):
                ph.wait("dve", "mx_part")
                ph.do("dve", lambda e, b: e.tensor_reduce(
                    mc[:, :].rearrange("p (h a q) -> p h a q", a=2, q=NQ)[:, :, 0, :], pmx[:, :, :, :],
                    AX.X, ALU.max), "mx_all")

            def shift(ph):
                k = bank(ph, "act")
                ph.wait("pe", "mx_all")
                ph.do("pe", lambda e, b: e.transpose(pm[0:64, k, 0:128], mc[:, :], ident[:, :]), "mx_t",
                      alone=True)
                ph.wait("act", "mx_t", "mrow0", "mrow1")
                ph.do("act", lambda e, b: e.activation(mr[:, 0, :], pm[0:64, k, 0:128], ACT.Copy, scale=-1.0), "mr0")
                ph.wait("dve", "mr0", "mx_t", "mrow0", "mrow1")
                ph.do("dve", lambda e, b: e.scalar_tensor_tensor(
                    out=mr[:, 1, :], in0=pm[0:64, k, 0:128], scalar=-1.0, in1=mr[:, 0, :],
                    op0=ALU.mult, op1=ALU.subtract), "mr")
                freed(ph, k, "mr")
                ph.wait("sp", "mr", f"scores{ch}")
                for i in range(2):
                    ph.do("sp", lambda e, b, i=i: e.dma_start(
                        qst[ch][KR + i:KR + i + 1, :, :].rearrange("o t c -> o (t c)"),
                        mr[:, i, :]), f"mrow{ch}", sem=f"mrow{ch}", by=16)

            return [whole, shift]

        slots = [(kind, v, kt) for v in range(2)
                 for kind, kt in [("cross", kt) for kt in range(NCT)] + [("self", kt) for kt in range(NQ)]]

        def shape_of(slot):
            kind, v, kt = slot
            if kind == "cross":
                return (128 if kt < NCT - 1 else REST), 0, kt, T + 128 * kt
            return 128, 128 * kt, NCT + kt, 128 * kt

        def scores(ph, ch, n, pair):
            kind, v, kt = slot = slots[n]
            m, q0, _, k0 = shape_of(slot)
            qc = 0 if kind == "cross" else T
            tt = 2 * v + pair
            for p in range(2):
                j, k = 2 * pair + p, score_ring.n % SB
                score_ring.n += 1
                ph.wait("pe", f"exp{k}", f"mrow{ch}", f"q_{ch}", f"ck0_{ch}", f"ck3_{ch}")
                ph.do("pe", lambda e, b, k=k, p=p: e.matmul(
                    ps[0:m, k, q0:T], kst[ch][0:KR + 2, 4 * p + tt, k0:k0 + m],
                    qst[ch][0:KR + 2, 4 * p + tt, qc + q0:qc + T], start=True, stop=True), f"scores{ch}")
                ph.wait("act", f"scores{ch}", f"pv{n % 2}")
                ph.do("act", lambda e, b, k=k, j=j: e.activation(
                    prob[0:m, n % 2, j, q0:T], ps[0:m, k, q0:T], ACT.Exp, scale=SCALE), f"exp{k}")
                last = ph.named[f"exp{k}"]
            if pair == 1:
                ph.named["exp"] = ph.named[f"prob{n % 2}"] = last
                if kind == "self":
                    ph.wait("pool", "exp")
                    ph.do("pool", lambda e, b: e.affine_select(
                        out=prob[:, n % 2, :, q0:q0 + 128], in_=prob[:, n % 2, :, q0:q0 + 128],
                        compare_op=ALU.is_ge, fill=0.0, base=0, pattern=[[0, 4], [1, 128]],
                        channel_multiplier=-1), f"prob{n % 2}")

        def weighted(ph, ch, n):
            kind, v, kt = slot = slots[n]
            m, q0, vi, _ = shape_of(slot)
            g = 2 * ch + v
            last = kt == (NCT if kind == "cross" else NQ) - 1
            ph.wait("pe", f"prob{n % 2}", "vt")
            if kt == 0:
                ph.wait("pe", "outs")
            for j in range(4):
                hl = 4 * (j % 2) + 2 * v + j // 2
                ph.do("pe", lambda e, b, j=j, hl=hl: e.matmul(
                    po[32 * j:32 * j + 32, q0:T], vt[ch][0:m, VW * vi + VE * hl:VW * vi + VE * hl + 32], prob[0:m, n % 2, j, q0:T],
                    start=kt == 0, stop=last), f"pv{n % 2}" if j == 3 else None)
            ph.named[f"values{ch}"] = ph.named[f"pv{n % 2}"]
            if not last:
                return None
            i = 0 if kind == "cross" else 1
            ph.wait("act", f"pv{n % 2}", "y_mul")
            ph.do("act", lambda e, b: e.copy(oc[:, i, :], po[:, :]), "outs")
            if i == 0:
                return None
            ph.wait("pool", "outs")
            ph.do("pool", lambda e, b: e.dma_start(
                scr["dn1"], bass.AP(oc[:, :, :].tensor, D * 2 * T, [[32 * 2 * T, 4], [1, 2 * T]])),
                "dn1", sem="dn1", by=16)
            ph.wait("pool", "dn1", "inv")
            ph.do("pool", lambda e, b: e.dma_start(
                dsum[:, :], scr["dn1"].rearrange("j (r c) -> (j r) c", c=32)), "dc", sem="dc", by=16)

            def divide(ph):
                ph.wait("dve", "dc")
                ph.do("dve", lambda e, b: e.reciprocal(dsum[:, :], dsum[:, :]), "inv")
                ph.wait("pool", "inv")
                ph.do("pool", lambda e, b: e.dma_start(
                    scr["dn2"].rearrange("j (r c) -> (j r) c", c=32), dsum[:, :]), "dn2", sem="dn2", by=16)
                ph.wait("pool", "dn2", "y_mul")
                for j in range(4):
                    ph.do("pool", lambda e, b, j=j: e.dma_start(
                        den[32 * j:32 * j + 32, :, :].rearrange("p a n -> p (a n)"),
                        scr["dn2"][j, :].partition_broadcast(32)), "den", sem="den", by=16)
                ph.wait("pool", "den")
                ph.do("pool", lambda e, b: e.tensor_tensor(oc[:, :, :], oc[:, :, :], den[:, :, :], ALU.mult), "y_mul")
                ph.wait("pool", "y_mul", "y_read")
                ph.do("pool", lambda e, b: e.tensor_tensor(yg[:, g, :], oc[:, 0, :], oc[:, 1, :], ALU.add), "y_sum")
                ph.named["y_mul"] = ph.named["y_sum"]
            return divide

        def finish_items(d):
            out = []
            tiles = lambda dram, b: dram[bass.ds((b + d) * T, T), :].rearrange("(q p) c -> p q c", p=128)

            def start(ph):
                ph.wait("sp", "ct_read", "x1_out")
                ph.do("sp", lambda e, b: e.dma_start(xr[:, :, :], x[b + d].rearrange("(q p) c -> p q c", p=128)),
                      "xr", sem="xr", by=16)
                ph.wait("pool", "xr", "bpt")
                for q in range(NQ):
                    ph.do("pool", lambda e, b, q=q: e.tensor_tensor(xr[:, q, :], xr[:, q, :], bpt[:, :], ALU.add), "xrb")

            def outproj(q):
                def item(ph):
                    k = bank(ph, "dve")
                    ph.wait("pe", "y_sum")
                    for g in range(4):
                        ph.do("pe", lambda e, b, g=g: e.matmul(
                            pm[:, k, 0:C], yg[:, g, 128 * q:128 * q + 128], wp[:, g, :], start=g == 0, stop=g == 3),
                            "y_read" if g == 3 else None)
                    got = keep(ph, "y_read")

                    def second(ph):
                        ph.wait("dve", got, "xrb", "gates")
                        ph.do("dve", lambda e, b: e.scalar_tensor_tensor(
                            out=xr[:, q, :], in0=pm[:, k, 0:C], scalar=gates[:, 0:1], in1=xr[:, q, :],
                            op0=ALU.mult, op1=ALU.add), "x1")
                        freed(ph, k, "x1")
                        if q == NQ - 1:
                            row_stats(ph, xr, ("x1",))
                    return second
                return item

            def norm2(ph):
                normalise(ph, xr, xa, "xn2")
                ph.wait("sp", "xn2")
                ph.do("sp", lambda e, b: e.dma_start(tiles(scr["xn"], b), xa[:, :, :]),
                      "xn_out", sem="xn_out", by=16)

            def router(ph):
                k = bank(ph, "dve")
                ph.wait("pe", "xt")
                for q in range(NQ):
                    for kc in range(KC):
                        ph.do("pe", lambda e, b, q=q, kc=kc: e.matmul(
                            pm[:, k, E * q:E * q + E], xt[:, kc, 128 * q:128 * q + 128], wg[:, kc, :],
                            start=kc == 0, stop=kc == KC - 1), "xt_read" if q == NQ - 1 and kc == KC - 1 else None)
                ph.wait("dve", "xt_read", "lg_read")
                ph.do("dve", lambda e, b: e.tensor_copy(
                    lgt[:, :, :], pm[:, k, 0:E * NQ].rearrange("p (q e) -> p q e", e=E)), "lg")
                freed(ph, k, "lg")

            def hidden(m):
                def item(ph):
                    ka, kb = bank(ph, "dve"), bank(ph, "dve")
                    ph.wait("pe", "xt")
                    for k, wt in ((ka, ws1), (kb, ws3)):
                        for kc in range(KC):
                            ph.do("pe", lambda e, b, k=k, wt=wt, kc=kc: e.matmul(
                                pm[:, k, :], wt[:, kc, 128 * m:128 * m + 128], xt[:, kc, :],
                                start=kc == 0, stop=kc == KC - 1), "xt_read" if kc == KC - 1 else None)
                    ph.wait("act", "xt_read", "wr0", "wr1", "act_t")
                    ph.do("act", lambda e, b: e.activation(sig_t[:, 0, :], pm[:, ka, :], ACT.Tanh, scale=0.5), "tanh")
                    got = keep(ph, "tanh")

                    def second(ph):
                        ph.wait("dve", got)
                        ph.do("dve", lambda e, b: e.scalar_tensor_tensor(
                            out=sig_t[:, 1, :], in0=sig_t[:, 0, :], scalar=1.0, in1=pm[:, ka, :],
                            op0=ALU.add, op1=ALU.mult), "silu")
                        freed(ph, ka, "silu")
                        ph.wait("dve", "silu", "z_read")
                        ph.do("dve", lambda e, b: e.scalar_tensor_tensor(
                            out=act_t[:, m, :], in0=sig_t[:, 1, :], scalar=0.5, in1=pm[:, kb, :],
                            op0=ALU.mult, op1=ALU.mult), "act_t")
                        freed(ph, kb, "act_t")
                    return second
                return item

            def shared_out(q):
                def item(ph):
                    k = bank(ph, "dve")
                    ph.wait("pe", "act_t")
                    for m in range(KC):
                        ph.do("pe", lambda e, b, m=m: e.matmul(
                            pm[:, k, 0:C], act_t[:, m, 128 * q:128 * q + 128], ws2[:, m, :],
                            start=m == 0, stop=m == KC - 1), "z_read" if m == KC - 1 else None)
                    got = keep(ph, "z_read")

                    def second(ph):
                        ph.wait("dve", got, "x1", "ln_a")
                        ph.do("dve", lambda e, b: e.scalar_tensor_tensor(
                            out=xr[:, q, :], in0=pm[:, k, 0:C], scalar=gates[:, 1:2], in1=xr[:, q, :],
                            op0=ALU.mult, op1=ALU.add), "x1z")
                        freed(ph, k, "x1z")
                        if q == NQ - 1:
                            ph.wait("sp", "x1z")
                            ph.do("sp", lambda e, b: e.dma_start(tiles(scr["x1z"], b), xr[:, :, :]),
                                  "x1_out", sem="x1_out", by=16)
                    return second
                return item

            out.append(start)
            out += [outproj(q) for q in range(NQ)]
            out.append(norm2)
            out += [transpose_item(xa, "xn2", ("xt_read",), "xn2_t", kc) for kc in range(KC)]
            out.append(router)
            out += [hidden(m) for m in range(KC)]
            out += [shared_out(q) for q in range(NQ)]
            return out

        def route_items(d):
            v3 = lambda a: a.rearrange("p (q e) -> p q e", e=E)
            v4 = lambda a: a.rearrange("p (k f) -> p k f", k=K)
            by_q = lambda a: a.unsqueeze(2).broadcast_to([128, NQ, E])
            by_e = lambda a: a.unsqueeze(1).broadcast_to([128, NQ, E])

            def dve(ph, fn, name="step", *waits):
                ph.wait("dve", *waits, "step")
                ph.do("dve", fn, name)
                ph.named["step"] = ph.named["routed"] = ph.named[name]

            def fetch(ph):
                ph.wait("sp", "xn_out", "wr0", "wr1", "z_read", "sc")
                ph.do("sp", lambda e, b: e.dma_start(
                    xs.rearrange("p (q c) -> p q c", c=C), scr["xn"][bass.ds((b + d) * T, T), :].rearrange(
                        "(q p) c -> p q c", p=128)), "xs", sem="xs", by=16)

            def softmax_a(ph):
                dve(ph, lambda e, b: e.tensor_reduce(tot[:, 0:NQ], lgt[:, :, :], AX.X, ALU.max),
                    "step", "lg", "wr0", "wr1", "act_t", "sc")
                dve(ph, lambda e, b: e.tensor_tensor(v3(sm), lgt[:, :, :], by_q(tot[:, 0:NQ]), ALU.subtract), "lg_read")
                ph.wait("act", "lg_read")
                ph.do("act", lambda e, b: e.activation(sm, sm, ACT.Exp), "sm_exp")

            def softmax_b(ph):
                dve(ph, lambda e, b: e.tensor_reduce(tot[:, NQ:2 * NQ], v3(sm), AX.X, ALU.add), "step", "sm_exp")
                dve(ph, lambda e, b: e.reciprocal(tot[:, 2 * NQ:3 * NQ], tot[:, NQ:2 * NQ]))
                dve(ph, lambda e, b: e.tensor_tensor(v3(sm), v3(sm), by_q(tot[:, 2 * NQ:3 * NQ]), ALU.mult))

            def choose(k):
                ks = slice(NQ * k, NQ * k + NQ)
                hk = v3(hot[:, NQ * E * k:NQ * E * (k + 1)])

                def first_half(ph):
                    dve(ph, lambda e, b: e.tensor_reduce(wt[:, ks], v3(sm), AX.X, ALU.max))
                    dve(ph, lambda e, b: e.tensor_tensor(v3(eq), v3(sm), by_q(wt[:, ks]), ALU.is_equal))
                    dve(ph, lambda e, b: e.tensor_tensor(v3(eq), v3(eq), by_e(down[:, :]), ALU.mult))

                def second_half(ph):
                    dve(ph, lambda e, b: e.tensor_reduce(best[:, ks], v3(eq), AX.X, ALU.max))
                    dve(ph, lambda e, b: e.tensor_tensor(hk, by_e(down[:, :]), by_q(best[:, ks]), ALU.is_equal))
                    dve(ph, lambda e, b: e.scalar_tensor_tensor(
                        out=v3(sm), in0=hk, scalar=-2.0, in1=v3(sm), op0=ALU.mult, op1=ALU.add))
                    if k == K - 1:
                        dve(ph, lambda e, b: e.tensor_scalar(mem, sm, 0.0, None, ALU.is_lt), "mem")
                return [first_half, second_half]

            def rank(ph):
                k = bank(ph, "dve")
                ph.wait("pe", "mem")
                for q in range(NQ + 1):
                    for p in range(min(q, NQ - 1) + 1):
                        ph.do("pe", lambda e, b, q=q, p=p: e.matmul(
                            pm[:, k, E * q:E * q + E], (tri if p == q else ones)[:, :], mem[:, E * p:E * p + E],
                            start=p == 0, stop=p == min(q, NQ - 1)), "ranks" if q == NQ and p == NQ - 1 else None)
                dve(ph, lambda e, b: e.tensor_tensor(v3(place), v3(pm[:, k, 0:E * NQ]), by_e(cnt[:, :]), ALU.add),
                    "step", "ranks")
                dve(ph, lambda e, b: e.tensor_tensor(cnt[:, :], cnt[:, :], pm[:, k, E * NQ:E * NQ + E], ALU.add), "cnt")
                freed(ph, k, "cnt")

            def pick_rank(ph):
                dve(ph, lambda e, b: e.tensor_tensor(
                    v4(pick), v4(hot), place.unsqueeze(1).broadcast_to([128, K, NQ * E]), ALU.mult))
                dve(ph, lambda e, b: e.tensor_reduce(ok, v3(pick), AX.X, ALU.add))

            def to_rows(ph):
                dve(ph, lambda e, b: e.tensor_scalar(rowf, best, float(-stride), float(E * stride), ALU.mult, ALU.add))
                dve(ph, lambda e, b: e.tensor_tensor(rowf, rowf, ok, ALU.add))
                dve(ph, lambda e, b: e.tensor_scalar(ok, ok, float(cap), None, ALU.is_lt))
                dve(ph, lambda e, b: e.tensor_tensor(rowf, rowf, over[:, :], ALU.subtract))
                dve(ph, lambda e, b: e.tensor_tensor(rowf, rowf, ok, ALU.mult))

            def to_rows_b(ph):
                dve(ph, lambda e, b: e.tensor_tensor(rowf, rowf, over[:, :], ALU.add))
                dve(ph, lambda e, b: e.tensor_copy(rows[:, :], rowf), "rows", "sc", "rows_out")
                dve(ph, lambda e, b: e.tensor_scalar(wt, wt, gates[:, 1:2], None, ALU.mult))
                dve(ph, lambda e, b: e.tensor_tensor(wout[:, :], wt, ok, ALU.mult), "wout")
                ph.wait("sp", "rows", "wout")
                for dram, tile in ((scr["rows"], rows), (scr["wts"], wout)):
                    ph.do("sp", lambda e, b, dram=dram, tile=tile: e.dma_start(
                        dram[bass.ds(b + d, 1)].rearrange("o p c -> (o p) c"), tile[:, :]),
                        "rows_out", sem="rows_out", by=16)

            def scatter(q, k):
                def item(ph):
                    ph.wait("pool", "rows", "xs")
                    ph.do("pool", lambda e, b: e.indirect_dma_start(
                        scr["slots"], bass.IndirectOffsetOnAxis(ap=rows[:, NQ * k + q:NQ * k + q + 1].bitcast(U32), axis=0),
                        xs[:, C * q:C * q + C], None), "sc", sem="sc", by=16)
                return item

            steps = [fetch, softmax_a, softmax_b]
            for k in range(K):
                steps += choose(k)
            steps += [rank, pick_rank, to_rows, to_rows_b]
            return steps, [scatter(q, k) for q in range(NQ) for k in range(K)]

        def stats1(ph):
            row_stats(ph, xa, ("x",))

        def norm1(ph):
            normalise(ph, xa, xa, "ln1")

        def first_items():
            return [transpose_item(xa, "ln1", ("xt_read",), "ln1_t", kc) for kc in range(KC)]

        def deal(table, load, places, items, cost):
            for n, it in zip(places, items, strict=True):
                table.setdefault(n, []).append(it)
                load[n] = load.get(n, 0) + cost

        def fill(table, load, lo, hi, items, costs):
            level = (sum(costs) + sum(load.get(n, 0) for n in range(lo, hi))) / (hi - lo)
            i, due = 0, 0.0
            for n in range(lo, hi):
                due += level - load.get(n, 0)
                while i < len(items) and (due >= costs[i] / 2 or n == hi - 1):
                    table.setdefault(n, []).append(items[i])
                    due -= costs[i]
                    i += 1

        NS = len(slots)

        def half(ph, ch, table, pending):
            later, seconds = {}, []
            for n in range(NS):
                for fn in later.pop(n, []):
                    fn(ph)
                for pair in range(2):
                    scores(ph, ch, n, pair)
                    for second in seconds:
                        second(ph)
                    seconds = [f for f in [it(ph) for it in table.get(2 * n + pair, [])] if f]
                if pending is not None:
                    div = weighted(ph, *pending)
                    if div:
                        later.setdefault(n + 4, []).append(div)
                pending = (ch, n)
            assert not later and not seconds
            return pending

        def body(ph, first, last):
            t0, t1, l0, l1 = {}, {}, {}, {}
            operands0, values0 = project_items(0)
            operands1, values1 = project_items(1)
            end = 2 * NS - 5
            t0[0] = [stack_item(1)]
            deal(t0, l0, (0, 1, 2, 3, 4), values1, 1.35)
            if not first:
                fin = finish_items(-1)
                deal(t0, l0, (6, 16, 17, 18, 19, 22, 24, 25, 26), fin[:9], 0.9)
                deal(t0, l0, (28, 31), fin[9:11], 2.9)
                deal(t0, l0, (34, 35, 36, 37), fin[11:], 0.8)
            if not last:
                deal(t0, l0, (28, 40, 33, 36, 39, 40),
                     [lambda ph: load_x(ph, 1), lambda ph: load_ctx(ph, 1), stats1, norm1] + first_items(), 0.5)
                deal(t0, l0, (41, 44, 47, 51, 54, 57, 60), operands0, 1.8)
                t1[0] = [stack_item(0)]
                deal(t1, l1, (0, 1, 2, 3, 4), values0, 1.35)
                deal(t1, l1, range(34, 55, 3), operands1, 1.8)
            if not first:
                steps, copies = route_items(-1)
                deal(t1, l1, range(1, 1 + len(steps)), steps, 1.0)
                deal(t1, l1, range(16, 16 + len(copies)), copies, 0.0)
            if not last:
                fill(t1, l1, 4, end, *max_items(0))
                deal(t1, l1, (end, end + 1), shift_items(0), 0.3)
            fill(t0, l0, 4, end, *max_items(1))
            deal(t0, l0, (end, end + 1), shift_items(1), 0.3)
            pend = half(ph, 0, t0, None if first else (1, NS - 1))
            half(ph, 1, t1, pend)
            ring.n += -ring.n % RB
            score_ring.n += -score_ring.n % SB

        P = Phase()
        load_x(P, 0)
        load_ctx(P, 0)
        stats1(P)
        norm1(P)
        load_weights(P)
        operands, values = project_items(0)
        operands1, _ = project_items(1)
        run_all(P, first_items() + operands + [stack_item(0)] + values + max_items(0)[0] + shift_items(0) + operands1)
        for e in ENGINES:
            P.wait(e, "w", "gates", "bpt", "identb", "mask", "c2", "vt_ones", "st_ones", "rc")
        for k in ("w", "gates", "bpt", "ident", "identb", "mask", "c0", "c1", "c2", "vt_ones", "st_ones", "rc"):
            P.named.pop(k)
        F = Phase(P)
        body(F, True, False)
        M0 = Phase(F)
        body(M0, False, False)
        M = Phase(M0)
        body(M, False, False)
        L = Phase(M)
        body(L, False, True)
        X = Phase(L)
        div = weighted(X, 1, NS - 1)
        div(X)
        steps, copies = route_items(0)
        finish = finish_items(0)

        def experts(i, *after):
            def item(ph):
                ph.wait("act", "scores0", "scores1", "mx0", "mx1", *after)
                load_experts(ph, wall, w, i)
            return item

        run_all(X, finish[:2] + [experts(0, "y_sum")] + finish[2:6] + [experts(1, "xn2")] + finish[6:9]
                + [experts(2, "xn2_t")] + finish[9:11] + [experts(3, "xt_read")] + finish[11:] + steps + copies)
        X.wait("sp", "cnt")
        X.do("sp", lambda e, b: e.dma_start(scr["cnt"], cnt[0:1, :]), "cnt_out", sem="cnt_out", by=16)
        X.wait("sp", "x1_out", "xn_out", "rows_out", "sc", "cnt_out", "wall")

        assert B >= 3
        before_m = total(P, F)

        block = ctx.enter_context(nc.Block())

        def program(name):
            def emit(eng):
                P.run(name, eng, sems, {}, 0)
                F.run(name, eng, sems, total(P), 0)
                with eng.Fori(1, B - 1) as b:
                    base = {s: before_m.get(s, 0) + (b - 1) * M.count.get(s, 0) for s in names}
                    M.run(name, eng, sems, base, b)
                done = {s: before_m.get(s, 0) + (B - 2) * M.count.get(s, 0) for s in names}
                L.run(name, eng, sems, done, B - 1)
                done = {s: n + L.count.get(s, 0) for s, n in done.items()}
                X.run(name, eng, sems, done, B - 1)
            return emit

        block.tensor(program("pe"))
        block.scalar(program("act"))
        block.vector(program("dve"))
        block.gpsimd(program("pool"))
        block.sync(program("sp"))


def run_phases(nc, ctx, sems, first, body, last, count):
    block = ctx.enter_context(nc.Block())

    def program(name):
        def emit(eng):
            first.run(name, eng, sems, {}, 0)
            start = total(first)
            with eng.Fori(1, 1 + count) as i:
                base = {s: start.get(s, 0) + (i - 1) * body.count.get(s, 0) for s in sems}
                body.run(name, eng, sems, base, i)
            done = {s: start.get(s, 0) + count * body.count.get(s, 0) for s in sems}
            last.run(name, eng, sems, done, count + 1)
        return emit

    block.tensor(program("pe"))
    block.scalar(program("act"))
    block.vector(program("dve"))
    block.gpsimd(program("pool"))
    block.sync(program("sp"))


def build_experts(nc, B, w, scr, wall):
    E, C, H, KC, GR = 32, 256, 128, 2, 256
    tokens, cap, stride, groups, dump = limits(B)
    U = 4
    with ExitStack() as ctx:
        def sb(name, shape, dt=F32):
            return ctx.enter_context(nc.sbuf_tensor(name, shape, dt))
        we = [sb(f"e_we{i}", [128, 2 * KC * H + C]) for i in range(U)]
        ident = sb("e_ident", [128, 128])
        zero = sb("e_zero", [128, 2, C])
        xin = [sb(f"e_xin{i}", [128, 2, C]) for i in range(U)]
        xt = [sb(f"e_xt{i}", [128, KC, GR]) for i in range(2)]
        th = [sb(f"e_th{i}", [128, GR]) for i in range(2)]
        sl = [sb(f"e_sl{i}", [128, GR]) for i in range(2)]
        act = [sb(f"e_act{i}", [128, GR]) for i in range(2)]
        yo = [sb(f"e_yo{i}", [128, 2, C]) for i in range(2)]
        cnt = sb("e_cnt", [128, E])
        ncap = sb("e_ncap", [128, E])
        gend = sb("e_gend", [128, E])
        gtmp = sb("e_gtmp", [128, E])
        shift = sb("e_shift", [128, E])
        gint = sb("e_gint", [128, E], I32)
        firstz = sb("e_firstz", [128, E])
        zrow = sb("e_zrow", [128, E], I32)
        NC2 = -(-groups // 128)
        gid = sb("e_gid", [128, NC2])
        gcl = sb("e_gcl", [128, NC2])
        le = sb("e_le", [128, NC2, E])
        les = sb("e_les", [128, NC2, E])
        tab = sb("e_tab", [128, 2, NC2])
        tmp = sb("e_tmp", [128, 2, NC2])
        tabi = sb("e_tabi", [128, 2, NC2], I32)
        NT = NC2 * 128 + 4
        table = sb("e_table", [1, 2 * NT], I32)
        pt = [ctx.enter_context(nc.psum_tensor(f"e_pt{i}", [128, KC, GR], F32)) for i in range(2)]
        phd = [ctx.enter_context(nc.psum_tensor(f"e_ph{i}", [128, 2, GR], F32)) for i in range(2)]
        py = [ctx.enter_context(nc.psum_tensor(f"e_py{i}", [128, 2, C], F32)) for i in range(2)]
        names = list(ENGINES) + ["cnt", "tab", "tab2", "zf"] + [f"xin{i}" for i in range(U)] + ["yo0", "yo1"] \
            + [f"spare_{e}" for e in ENGINES]
        sems = {n: ctx.enter_context(nc.semaphore(f"e_{n}")) for n in names}

        def tables(ph):
            ph.do("sp", lambda e, b: e.dma_start(cnt[:, :], scr["cnt"][0, :].partition_broadcast(128)), "cnt", sem="cnt", by=16)

            def pool(fn, name="pstep"):
                ph.wait("pool", "pstep")
                ph.do("pool", fn, name)
                ph.named["pstep"] = ph.named[name]
            pool(lambda e, b: e.memset(ident[:, :], 0.0))
            pool(lambda e, b: e.affine_select(out=ident[:, :], in_=ident[:, :], compare_op=ALU.not_equal, fill=1.0,
                                              base=0, pattern=[[-1, 128]], channel_multiplier=1))
            pool(lambda e, b: e.iota(gid[:, :], pattern=[[128, NC2]], base=0, channel_multiplier=1,
                                     allow_small_or_imprecise_dtypes=True))
            pool(lambda e, b: e.iota(firstz[:, :], pattern=[[stride, E]], base=0, channel_multiplier=0,
                                     allow_small_or_imprecise_dtypes=True))
            ph.named["iotas"] = ph.named["pstep"]

            def dve(fn, *waits):
                ph.wait("dve", *waits, "step")
                ph.do("dve", fn, "step")
            dve(lambda e, b: e.memset(zero[:, :, :], 0.0))
            dve(lambda e, b: e.memset(table[:, :], 0))
            dve(lambda e, b: e.tensor_scalar(ncap[:, :], cnt[:, :], float(cap), None, ALU.min), "cnt")
            dve(lambda e, b: e.tensor_tensor(zrow[:, :], ncap[:, :], firstz[:, :], ALU.add), "iotas")
            ph.named["zrow"] = ph.named["step"]
            dve(lambda e, b: e.tensor_scalar(gint[:, :], ncap[:, :], float(GR - 1), None, ALU.add))
            dve(lambda e, b: e.tensor_scalar(gint[:, :], gint[:, :], 8, None, ALU.arith_shift_right))
            dve(lambda e, b: e.tensor_copy(gend[:, :], gint[:, :]))
            dve(lambda e, b: e.memset(shift[:, :], 0.0))
            dve(lambda e, b: e.tensor_scalar(shift[:, 1:E], gend[:, 0:E - 1], float(GR), float(-stride), ALU.mult, ALU.add))
            ph.named["shift"] = ph.named["step"]
            a, o = gend, gtmp
            n = 1
            while n < E:
                dve(lambda e, b, a=a, o=o, n=n: e.tensor_tensor(o[:, n:E], a[:, n:E], a[:, 0:E - n], ALU.add))
                dve(lambda e, b, a=a, o=o, n=n: e.tensor_copy(o[:, 0:n], a[:, 0:n]))
                a, o, n = o, a, 2 * n
            gsum = a
            last = gsum[:, E - 1:E]
            dve(lambda e, b: e.tensor_scalar(gcl[:, :], gid[:, :], 1.0, last, ALU.add, ALU.min))
            dve(lambda e, b: e.tensor_scalar(gcl[:, :], gcl[:, :], -1.0, None, ALU.add))
            bc = lambda v: v.unsqueeze(2).broadcast_to([128, NC2, E])
            per = lambda v: v.unsqueeze(1).broadcast_to([128, NC2, E])
            dve(lambda e, b: e.tensor_tensor(le[:, :, :], per(gsum[:, :]), bc(gcl[:, :]), ALU.is_le))
            dve(lambda e, b: e.tensor_tensor(les[:, :, :], le[:, :, :], per(gsum[:, :]), ALU.mult))
            dve(lambda e, b: e.tensor_reduce(tab[:, 0, :], le[:, :, :], AX.X, ALU.add))
            dve(lambda e, b: e.tensor_reduce(tmp[:, 0, :], les[:, :, :], AX.X, ALU.max))
            dve(lambda e, b: e.tensor_tensor(tmp[:, 0, :], gcl[:, :], tmp[:, 0, :], ALU.subtract))
            dve(lambda e, b: e.tensor_scalar(tmp[:, 0, :], tmp[:, 0, :], float(GR), None, ALU.mult))
            dve(lambda e, b: e.tensor_scalar(tmp[:, 1, :], tab[:, 0, :], float(stride), None, ALU.mult))
            dve(lambda e, b: e.tensor_tensor(tab[:, 1, :], tmp[:, 0, :], tmp[:, 1, :], ALU.add))
            dve(lambda e, b: e.tensor_copy(tabi[:, :, :], tab[:, :, :]))
            ph.named["tab"] = ph.named["step"]
            ph.wait("sp", "zrow")

            starts = {}

            def fill(e, x):
                if x % 8 == 0:
                    _, starts["now"] = nc.values_load_multi_w_load_instructions(
                        zrow[0:1, x:x + 8], engines=[mybir.EngineType.SP], min_val=0, max_val=dump - 1)
                return e.dma_start(scr["slots"][bass.ds(starts["now"][x % 8], GR), :].rearrange("(q p) c -> p q c", p=128),
                                   zero[:, :, :])

            def fills(lo, hi):
                for x in range(lo, hi):
                    ph.do("sp", lambda e, b, x=x: fill(e, x), "zf", sem="zf", by=16)

            fills(0, E // 2)
            ph.wait("sp", "shift", "tab")
            ph.do("sp", lambda e, b: e.dma_start(scr["shift"], shift[0:1, :]), "zf", sem="zf", by=16)
            ph.do("sp", lambda e, b: e.dma_start(scr["tab"].rearrange("k c p -> p k c"), tabi[:, :, :],
                                                 allow_slow_non_contiguous=True), "tab1", sem="tab", by=16)
            fills(E // 2, E)
            ph.wait("sp", "tab1")
            for k, at in ((0, 1), (1, NT)):
                ph.do("sp", lambda e, b, k=k, at=at: e.dma_start(
                    table[:, at:at + NC2 * 128], scr["tab"][k].rearrange("c p -> (c p)").unsqueeze(0)),
                    "table", sem="tab2", by=16)
            ph.wait("sp", "zf", "table")
            ph.wait("pe", "iotas")
            ph.wait("act", "table")

        held = {}

        def entry(e, engine, k, b, d, hi):
            at = d + (1 if k == 0 else 0)
            if at % U == 0 or engine not in held:
                at -= at % U
                _, held[engine] = nc.values_load_multi_w_load_instructions(
                    table[0:1, bass.ds(U * b + at + k * NT, U)], engines=[engine], min_val=0, max_val=hi)
            return held[engine][(d + (1 if k == 0 else 0)) % U]

        def load(ph, u, d):
            ph.wait("sp", f"xr{u}")
            def go(e, b):
                row = entry(e, mybir.EngineType.SP, 1, b, d, dump - GR)
                return e.dma_start(xin[u][:, :, :], scr["slots"][bass.ds(row, GR), :].rearrange("(q p) c -> p q c", p=128))
            ph.do("sp", go, f"xin{u}", sem=f"xin{u}", by=16)

        def transposes(ph, u):
            i = u % 2
            ph.wait("pe", f"xin{u}", f"xt{i}")
            for kc in range(KC):
                for q in range(2):
                    ph.do("pe", lambda e, b, kc=kc, q=q: e.transpose(
                        pt[i][:, kc, 128 * q:128 * q + 128], xin[u][:, q, 128 * kc:128 * kc + 128], ident[:, :]),
                        f"xr{u}" if kc and q else None)
            ph.wait("act", f"xr{u}", f"h{i}")
            ph.do("act", lambda e, b: e.copy(xt[i][:, :, :], pt[i][:, :, :]), f"xt{i}")

        def weights(ph, u, d):
            ph.wait("act", f"y_of{u}")

            def go(e, b):
                x = entry(e, mybir.EngineType.Activation, 0, b, d, E - 1)
                return e.copy(we[u][:, :], wall[:, bass.ds(x, 1), :].rearrange("p o c -> p (o c)"))
            ph.do("act", go, f"we{u}")

        def hidden(ph, u, d):
            i = u % 2
            ph.wait("pe", f"xt{i}", f"we{u}", f"act{i}")
            for m in range(2):
                for kc in range(KC):
                    c0 = H * (KC * m + kc)
                    ph.do("pe", lambda e, b, m=m, kc=kc, c0=c0: e.matmul(
                        phd[i][:, m, :], we[u][:, c0:c0 + H], xt[i][:, kc, :], start=kc == 0, stop=kc == KC - 1),
                        f"h{i}" if m and kc == KC - 1 else None)
            ph.wait("act", f"h{i}", f"sl{i}")
            ph.do("act", lambda e, b: e.activation(th[i][:, :], phd[i][:, 0, :], ACT.Tanh, scale=0.5), f"th{i}")
            ph.wait("dve", f"th{i}", f"act{i}")
            ph.do("dve", lambda e, b: e.scalar_tensor_tensor(
                out=sl[i][:, :], in0=th[i][:, :], scalar=1.0, in1=phd[i][:, 0, :], op0=ALU.add, op1=ALU.mult), f"sl{i}")
            ph.wait("dve", f"sl{i}", f"y{i}")
            ph.do("dve", lambda e, b: e.scalar_tensor_tensor(
                out=act[i][:, :], in0=sl[i][:, :], scalar=0.5, in1=phd[i][:, 1, :], op0=ALU.mult, op1=ALU.mult), f"act{i}")

        def outs(ph, u, d):
            i = u % 2
            ph.wait("pe", f"act{i}", f"yc{i}")

            for q in range(2):
                ph.do("pe", lambda e, b, q=q: e.matmul(
                    py[i][:, q, :], act[i][:, 128 * q:128 * q + 128], we[u][:, 2 * KC * H:], start=True, stop=True),
                    f"y{i}" if q else None)
            ph.named[f"y_of{u}"] = ph.named[f"y{i}"]
            ph.wait("dve", f"y{i}", f"yo{i}")
            ph.do("dve", lambda e, b: e.tensor_copy(yo[i][:, :, :], py[i][:, :, :]), f"yc{i}")
            ph.wait("sp", f"yc{i}")

            ph.do("sp", lambda e, b: e.dma_start(
                scr["outs"][bass.ds((4 * b + d) * GR, GR), :].rearrange("(q p) c -> p q c", p=128), yo[i][:, :, :]),
                f"yo{i}", sem=f"yo{i}", by=16)

        def turn(ph, first, last):
            for u in range(U):
                hidden(ph, u, u)
                if not last or u < U - 1:
                    transposes(ph, (u + 1) % U)
                if not (first and u == 0):
                    outs(ph, (u - 1) % U, u - 1)
                if not last or u < U - 3:
                    weights(ph, (u + 3) % U, u + 3)
                if not last:
                    load(ph, u, u + U)

        F = Phase()
        tables(F)
        for u in range(U):
            load(F, u, u)
        for e in ENGINES:
            if e != "sp":
                F.wait(e, "table")
        for k in ("table", "iotas", "zf"):
            F.named.pop(k)
        for u in range(3):
            weights(F, u, u)
        transposes(F, 0)
        turn(F, True, False)
        M0 = Phase(F)
        turn(M0, False, False)
        M = Phase(M0)
        turn(M, False, False)
        X = Phase(M)
        turn(X, False, True)
        outs(X, U - 1, U - 1)
        X.wait("sp", "yo0", "yo1")
        run_phases(nc, ctx, sems, F, M, X, groups // U - 2)


def build_combine(nc, B, w, scr, out):
    NQ, K, C = 4, 4, 256
    with ExitStack() as ctx:
        def sb(name, shape, dt=F32):
            return ctx.enter_context(nc.sbuf_tensor(name, shape, dt))
        E, GR = 32, 256
        tokens, cap, stride, groups, dump = limits(B)
        rows = [sb(f"c_rows{i}", [128, K * NQ], I32) for i in range(2)]
        gidx = [sb(f"c_gidx{i}", [128, K * NQ], I32) for i in range(2)]
        rowf = sb("c_rowf", [128, K * NQ])
        add_ = sb("c_add", [128, K * NQ])
        ge = sb("c_ge", [128, K * NQ, E])
        shift = sb("c_shift", [128, E])
        first_row = sb("c_first", [128, E])
        wt = [sb(f"c_wt{i}", [128, K * NQ]) for i in range(2)]
        acc = [sb(f"c_acc{i}", [128, NQ, C]) for i in range(2)]
        got = [sb(f"c_got{i}", [128, NQ, K, C]) for i in range(2)]
        names = list(ENGINES) + ["in0", "in1", "acc0", "acc1", "got0", "got1", "res0", "res1", "shift"] + [f"spare_{e}" for e in ENGINES]
        sems = {n: ctx.enter_context(nc.semaphore(f"c_{n}")) for n in names}
        view = lambda dram, b: dram[bass.ds(b * 512, 512), :].rearrange("(q p) c -> p q c", p=128)

        def load(ph, d, i):
            ph.wait("sp", f"idx{i}", f"sum{i}")
            ph.do("sp", lambda e, b: e.dma_start(rows[i][:, :], scr["rows"][bass.ds(2 * b + d, 1)].rearrange("o p c -> (o p) c")),
                  f"in{i}", sem=f"in{i}", by=16)
            ph.do("sp", lambda e, b: e.dma_start(wt[i][:, :], scr["wts"][bass.ds(2 * b + d, 1)].rearrange("o p c -> (o p) c")),
                  f"in{i}", sem=f"in{i}", by=16)
            ph.wait("sp", f"res{i}")
            ph.do("sp", lambda e, b: e.dma_start(acc[i][:, :, :], view(scr["x1z"], 2 * b + d)), f"acc{i}", sem=f"acc{i}", by=16)

        def gather(ph, i):
            ph.wait("dve", "step", f"in{i}")
            ph.do("dve", lambda e, b: e.tensor_copy(rowf[:, :], rows[i][:, :]), "step")
            ph.wait("dve", "step", "shift", "first")
            wide = [128, K * NQ, E]
            ph.do("dve", lambda e, b: e.tensor_tensor(
                ge[:, :, :], rowf[:, :].unsqueeze(2).broadcast_to(wide), first_row[:, :].unsqueeze(1).broadcast_to(wide),
                ALU.is_ge), "step")
            ph.wait("dve", "step")
            ph.do("dve", lambda e, b: e.tensor_tensor(
                ge[:, :, :], ge[:, :, :], shift[:, :].unsqueeze(1).broadcast_to(wide), ALU.mult), "step")
            ph.wait("dve", "step")
            ph.do("dve", lambda e, b: e.tensor_reduce(add_[:, :], ge[:, :, :], AX.X, ALU.add), "step")
            ph.wait("dve", "step")
            ph.do("dve", lambda e, b: e.tensor_tensor(rowf[:, :], rowf[:, :], add_[:, :], ALU.add), "step")
            ph.wait("dve", "step", f"got{i}")
            ph.do("dve", lambda e, b: e.tensor_scalar(
                gidx[i][:, :], rowf[:, :], float(GR * groups - 1), None, ALU.min), f"idx{i}")
            ph.named["step"] = ph.named[f"idx{i}"]
            ph.wait("pool", f"idx{i}", f"sum{i}")
            for q in range(NQ):
                for k in range(K):
                    ph.do("pool", lambda e, b, q=q, k=k: e.indirect_dma_start(
                        got[i][:, q, k, :], None, scr["outs"],
                        bass.IndirectOffsetOnAxis(ap=gidx[i][:, k * NQ + q:k * NQ + q + 1].bitcast(U32), axis=0)),
                        f"got{i}", sem=f"got{i}", by=16)

        def add(ph, d, i):
            ph.wait("dve", f"got{i}", f"acc{i}", f"in{i}")
            for k in range(K):
                for q in range(NQ):
                    ph.do("dve", lambda e, b, q=q, k=k: e.scalar_tensor_tensor(
                        out=acc[i][:, q, :], in0=got[i][:, q, k, :], scalar=wt[i][:, k * NQ + q:k * NQ + q + 1],
                        in1=acc[i][:, q, :], op0=ALU.mult, op1=ALU.add), f"sum{i}")
                if k < K - 1:
                    ph.wait("dve", f"sum{i}")
            ph.wait("sp", f"sum{i}")
            ph.do("sp", lambda e, b: e.dma_start(view(out, 2 * b + d), acc[i][:, :, :]), f"res{i}", sem=f"res{i}", by=16)

        F = Phase()
        load(F, 0, 0)
        load(F, 1, 1)
        F.do("sp", lambda e, b: e.dma_start(shift[:, :], scr["shift"][0, :].partition_broadcast(128)), "shift", sem="shift", by=16)
        F.do("pool", lambda e, b: e.iota(first_row[:, :], pattern=[[stride, E]], base=0, channel_multiplier=0,
                                         allow_small_or_imprecise_dtypes=True), "first")
        gather(F, 0)
        F.named.pop("shift")
        F.named.pop("first")

        def turn(ph, more):
            gather(ph, 1)
            add(ph, 0, 0)
            if more:
                load(ph, 2, 0)
                gather(ph, 0)
            add(ph, 1, 1)
            if more:
                load(ph, 3, 1)
        turn(F, True)
        M0 = Phase(F)
        turn(M0, True)
        M = Phase(M0)
        turn(M, True)
        X = Phase(M)
        turn(X, False)
        X.wait("sp", "res0", "res1")
        run_phases(nc, ctx, sems, F, M, X, B // 2 - 2)


def build(nc, arrays, out):
    x, ctx_t = arrays["x"], arrays["ctx_t"]
    B, T, C = x.shape
    w = {k.split("_")[-1]: a for k, a in arrays.items() if k.startswith("L0_")}
    w["g_xattn"], w["g_ffn"] = arrays["g_xattn"], arrays["g_ffn"]
    E = w["Wg"].shape[1]
    tokens, cap, stride, groups, dump = limits(B)

    def dram(name, shape, dt=F32):
        return nc.dram_tensor(f"scratch_{name}", shape, dt, kind="Internal").ap()

    scr = {
        "x1z": dram("x1z", [B * T, C]),
        "xn": dram("xn", [B * T, C]),
        "dn1": dram("dn1", [4, 2 * T]),
        "dn2": dram("dn2", [4, 2 * T]),
        "parts": dram("parts", [3, 3, 128, 1090], BF16),
        "slots": dram("slots", [dump + 2 * 128 * 16, C]),
        "outs": dram("outs", [256 * groups, C]),
        "rows": dram("rows", [B, 128, 16], I32),
        "wts": dram("wts", [B, 128, 16]),
        "cnt": dram("cnt", [1, E]),
        "shift": dram("shift", [1, E]),
        "tab": dram("tab", [2, -(-groups // 128), 128], I32),
    }
    with ExitStack() as ctx:
        TC, W = ctx_t.shape[2], 4 * 128 + C
        stacks = ctx.enter_context(nc.sbuf_tensor("stacks", [128, 2 * 8 * (3 * T + TC + 1)], BF16))
        wall = stacks[:, 0:2 * E * W].bitcast(F32).rearrange("p (e n) -> p e n", e=E)
        build_attention(nc, B, x, ctx_t, w, scr, stacks, wall)
        build_experts(nc, B, w, scr, wall)
    build_combine(nc, B, w, scr, out)


def kernel(**inputs):
    import concourse.bacc as bacc
    from concourse.bass_utils import run_bass_kernel_spmd

    nc = bacc.Bacc("TRN2", target_bir_lowering=False, num_devices=1)
    data, args = {}, {}
    for name, value in inputs.items():
        value = np.asarray(value)
        if name == "ctx_512":
            name, value = "ctx_t", value.transpose(0, 2, 1)
        data[f"in_{name}_dram"] = np.ascontiguousarray(value)
        args[name] = nc.dram_tensor(f"in_{name}_dram", value.shape, F32, kind="ExternalInput").ap()
    shape = inputs["x"].shape
    out = nc.dram_tensor("out_0_dram", (shape[0] * shape[1], shape[2]), F32, kind="ExternalOutput").ap()
    build(nc, args, out)
    nc.compile()
    result = run_bass_kernel_spmd(nc, [data], core_ids=[0])
    return result.results[0]["out_0_dram"].reshape(shape)
```
